# Optimizing a Trainium2 kernel written in Bass

```python
import numpy as np
import jax
import jax.numpy as jnp

def _softmax(x, axis=-1):
    return jax.nn.softmax(x, axis=axis)

def _gelu(x):
    return jax.nn.gelu(x, approximate=True)

def _silu(x):
    return jax.nn.silu(x)

def _sigmoid(x):
    return jax.nn.sigmoid(x)

def _layernorm(x, axis=-1, eps=1e-05):
    m = jnp.mean(x, axis=axis, keepdims=True)
    v = jnp.var(x, axis=axis, keepdims=True)
    return (x - m) / jnp.sqrt(v + eps)

def _scatter_add(tgt, idx, src, axis=0):
    return tgt.at[idx].add(src)

def _segment_sum(src, seg, n):
    return jax.ops.segment_sum(src, seg, n)
kernel_name = 'mk_gnn_resnorm_d2_gnn_r8_2a0757'

def setup_inputs(seed: int=0):
    np.random.seed(seed)
    _w = jnp.asarray

    def _rec_inputs():
        import jax
        import jax.numpy as jnp
        _gk = jax.random.key(seed)
        x = -0.000202 + 1 * jax.random.normal(jax.random.fold_in(_gk, 1), (12500, 128), jnp.float32)
        src = jax.random.randint(jax.random.fold_in(_gk, 2), (200000,), 0, 12500, jnp.int32)
        dst = jax.random.randint(jax.random.fold_in(_gk, 3), (200000,), 0, 12500, jnp.int32)
        _o = jnp.argsort(dst, stable=True)
        src = src[_o]
        dst = dst[_o]
        edge_attr_128 = -4.21973e-05 + 0.999841 * jax.random.normal(jax.random.fold_in(_gk, 12), (200000, 128), jnp.float32)
        return (x, src, dst, edge_attr_128)
    x, src, dst, edge_attr_128 = _rec_inputs()

    def _L0_gnn_setup():
        import jax, jax.numpy as jnp
        import numpy as np
        N_NODES = 6250
        N_EDGES = 100000
        IN_DIM = 128
        HEADS = 4
        C = 32
        HID = HEADS * C
        NEG_SLOPE = 0.2
        LN_EPS = 1e-05
        key = jax.random.key(seed)
        ks = jax.random.split(key, 6)
        x = jax.random.normal(ks[0], (N_NODES, IN_DIM), dtype=jnp.float32)
        edge_index = jax.random.randint(ks[1], (2, N_EDGES), 0, N_NODES, dtype=jnp.int64)
        scale = 1.0 / np.sqrt(IN_DIM)
        W_l = jax.random.normal(ks[2], (IN_DIM, HID), dtype=jnp.float32) * scale
        W_r = jax.random.normal(ks[3], (IN_DIM, HID), dtype=jnp.float32) * scale
        att = jax.random.normal(ks[4], (HEADS, C), dtype=jnp.float32) * (1.0 / np.sqrt(C))
        bias = jnp.zeros((HID,), dtype=jnp.float32)
        ln_gamma = jnp.ones((HID,), dtype=jnp.float32)
        ln_beta = jnp.zeros((HID,), dtype=jnp.float32)
        return {'x': x, 'edge_index': edge_index, 'W_l': W_l, 'W_r': W_r, 'att': att, 'bias': bias, 'ln_gamma': ln_gamma, 'ln_beta': ln_beta}
    _L0_gnn_all = _L0_gnn_setup()
    _L0_gnn_in = {k: v for k, v in _L0_gnn_all.items() if k in ('W_l', 'W_r', 'att', 'bias', 'ln_gamma', 'ln_beta')}
    del _L0_gnn_all

    def _L1_gnn_setup():
        import jax, jax.numpy as jnp
        import numpy as np
        N_NODES = 12500
        N_EDGES = 75000
        D = 128
        key = jax.random.key(seed)
        ks = jax.random.split(key, 6)
        node_feat = jax.random.normal(ks[0], (N_NODES, D), dtype=jnp.float32)
        edge_feat = jax.random.normal(ks[1], (N_EDGES, D), dtype=jnp.float32)
        src = jax.random.randint(ks[2], (N_EDGES,), 0, N_NODES, dtype=jnp.int32)
        dst = jax.random.randint(ks[3], (N_EDGES,), 0, N_NODES, dtype=jnp.int32)
        lim = 1.0 / np.sqrt(D)
        W1 = jax.random.uniform(ks[4], (D, D), jnp.float32, -lim, lim)
        b1 = jnp.zeros((D,), jnp.float32)
        W2 = jax.random.uniform(ks[5], (D, D), jnp.float32, -lim, lim)
        b2 = jnp.zeros((D,), jnp.float32)
        return {'node_feat': node_feat, 'edge_feat': edge_feat, 'src': src, 'dst': dst, 'W1': W1, 'b1': b1, 'W2': W2, 'b2': b2}
    _L1_gnn_all = _L1_gnn_setup()
    _L1_gnn_in = {k: v for k, v in _L1_gnn_all.items() if k in ('W1', 'b1', 'W2', 'b2')}
    del _L1_gnn_all
    return {'x': x, 'src': src, 'dst': dst, 'edge_attr_128': edge_attr_128, 'L0_gnn_W_l': _L0_gnn_in['W_l'], 'L0_gnn_W_r': _L0_gnn_in['W_r'], 'L0_gnn_att': _L0_gnn_in['att'], 'L0_gnn_bias': _L0_gnn_in['bias'], 'L0_gnn_ln_gamma': _L0_gnn_in['ln_gamma'], 'L0_gnn_ln_beta': _L0_gnn_in['ln_beta'], 'L1_gnn_W1': _L1_gnn_in['W1'], 'L1_gnn_b1': _L1_gnn_in['b1'], 'L1_gnn_W2': _L1_gnn_in['W2'], 'L1_gnn_b2': _L1_gnn_in['b2']}

def reference(x, src, dst, edge_attr_128, L0_gnn_W_l, L0_gnn_W_r, L0_gnn_att, L0_gnn_bias, L0_gnn_ln_gamma, L0_gnn_ln_beta, L1_gnn_W1, L1_gnn_b1, L1_gnn_W2, L1_gnn_b2):
    import jax
    import jax.numpy as jnp

    def _L0_gnn_ref(x, edge_index, W_l, W_r, att, bias, ln_gamma, ln_beta):
        import jax, jax.numpy as jnp
        import numpy as np
        N_NODES = 6250
        N_EDGES = 100000
        IN_DIM = 128
        HEADS = 4
        C = 32
        HID = HEADS * C
        NEG_SLOPE = 0.2
        LN_EPS = 1e-05
        N = x.shape[0]
        loops = jnp.arange(N, dtype=edge_index.dtype)
        ei = jnp.concatenate([edge_index, jnp.stack([loops, loops])], axis=1)
        src, dst = (ei[0], ei[1])
        xl = (x @ W_l).reshape(N, HEADS, C)
        xr = (x @ W_r).reshape(N, HEADS, C)
        h = xl[src] + xr[dst]
        e = jnp.einsum('ehc,hc->eh', jax.nn.leaky_relu(h, NEG_SLOPE), att)
        emax = jax.ops.segment_max(e, dst, num_segments=N)
        emax = jnp.where(jnp.isfinite(emax), emax, 0.0)
        p = jnp.exp(e - emax[dst])
        denom = jax.ops.segment_sum(p, dst, num_segments=N)
        alpha = p / denom[dst]
        msg = alpha[:, :, None] * xl[src]
        out = jax.ops.segment_sum(msg, dst, num_segments=N).reshape(N, HID) + bias
        out = out + x
        mean = jnp.mean(out, axis=-1, keepdims=True)
        var = jnp.var(out, axis=-1, keepdims=True)
        return (out - mean) * jax.lax.rsqrt(var + LN_EPS) * ln_gamma + ln_beta

    def _L1_gnn_ref(node_feat, edge_feat, src, dst, W1, b1, W2, b2):
        import jax, jax.numpy as jnp
        import numpy as np
        N_NODES = 12500
        N_EDGES = 75000
        D = 128
        m = node_feat[src] + edge_feat
        neigh = jax.ops.segment_sum(m, dst, num_segments=node_feat.shape[0])
        h = 2.0 * node_feat + neigh
        h = h @ W1 + b1
        h = jnp.where(h > 0, h, 0.01 * h)
        return h @ W2 + b2
    edge_index = jnp.stack([src, dst])
    x = _layernorm(x + _L0_gnn_ref(x, edge_index, L0_gnn_W_l, L0_gnn_W_r, L0_gnn_att, L0_gnn_bias, L0_gnn_ln_gamma, L0_gnn_ln_beta), axis=-1)
    x = _layernorm(x + _L1_gnn_ref(x, edge_attr_128, src, dst, L1_gnn_W1, L1_gnn_b1, L1_gnn_W2, L1_gnn_b2), axis=-1)
    return x

_drawn_inputs = setup_inputs


def setup_inputs(seed=0):
    import zlib

    import numpy as np

    out = dict(_drawn_inputs(seed))
    spreads = {'L0_gnn_bias': (0.0, 0.1),
     'L0_gnn_ln_gamma': (1.0, 0.2),
     'L0_gnn_ln_beta': (0.0, 0.1),
     'L1_gnn_b1': (0.0, 0.326),
     'L1_gnn_b2': (0.0, 0.1)}
    factors = {}
    for name, (base, spread) in spreads.items():
        noise = np.random.default_rng([zlib.crc32(name.encode()), seed]).standard_normal(out[name].shape)
        drawn = base * np.exp(spread * noise) if base else spread * noise
        out[name] = jnp.asarray(drawn.astype(out[name].dtype))
    for name, factor in factors.items():
        out[name] = (out[name] * factor).astype(out[name].dtype)
    return out
```

```python
from contextlib import ExitStack

import concourse.bass as bass
from concourse import mybir

F32 = mybir.dt.float32
I32 = mybir.dt.int32
ALU = mybir.AluOpType
ACT = mybir.ActivationFunctionType
AX = mybir.AxisListType

P = 128
D = 128
H = 4
C = D // H
T = 8
G = P * T
U = 4
UP = 7
HC = C + 1
WC = H * HC + H
WX = WC + 2 * H
BIG = 2.0 ** 112
GAT_SLOPE, MLP_SLOPE, EPS = 0.2, 0.01, 1e-5
SOFT_LINKS = 9


class Group:

    def __init__(self, j, c):
        self.j, self.c = j, c

    def __add__(self, n):
        return Group(self.j, self.c + n)

    def times(self, a, b=0):
        return a * self.c + b if self.j is None else self.j * (U * a) + (a * self.c + b)

    def use(self, a, b):
        return a * (self.c // U) + b if self.j is None else self.j * a + (a * (self.c // U) + b)

    def at_least(self, n):
        return self.j is not None or self.c >= n


def sweep(eng, groups, step, ends=None, layer=0):

    def part(tag, j, first, steps, lo, n):
        regs = []
        if ends is not None:
            regs = [eng.alloc_register(f"ends{layer}_{tag}_{k}") for k in range(2 * n)]
            eng.load(regs, ends[0:1, bass.ds(2 * first if j is None else j * (2 * U), 2 * n)])
        for c in steps:
            step(Group(j, c), lambda g: (regs[2 * (g.c - lo)], regs[2 * (g.c - lo) + 1]))

    part("head", None, 0, [0], 0, 2)
    with eng.Fori(0, groups // U - 1) as j:
        part("body", j, 0, range(1, U + 1), 0, U + 2)
    base = groups - U
    part("tail", None, base, range(base + 1, groups + 1), base, U)


def further_visits(eng, block, ends, body):
    first, last = ends
    eng.reg_add(block, first, 1)
    with eng.While(lambda: eng.snap(block) <= eng.snap(last)):
        body()
        eng.reg_add(block, block, 1)


def wait_alone(eng, waits, sem, value):
    eng.wait_ge(sem, value)
    eng.sem_inc(waits, 1)


class Chain:

    def __init__(self, eng, sem):
        self.eng, self.sem, self.base, self.n = eng, sem, 0, 0

    def at(self, base):
        self.base, self.n = base, 0

    def mark(self, ins):
        self.n += 1
        ins.then_inc(self.sem, 1)

    def link(self, ins):
        self.mark(ins)
        self.eng.wait_ge(self.sem, self.base + self.n)


def build(nc, a, out, edges, groups, blocks):
    nodes = blocks * P
    pairs = blocks // 2
    assert groups % U == 0 and groups > U and pairs % UP == 0
    assert edges % T == 0 and 0 < groups * G - edges < G
    ctx = ExitStack()
    with ctx:
        def sb(name, shape, dt=F32):
            return ctx.enter_context(nc.sbuf_tensor(name, shape, dt))

        def pb(name, shape):
            return ctx.enter_context(nc.psum_tensor(name, shape, F32))

        xl_table = nc.dram_tensor("xl_table", (nodes, D), F32, kind="Internal").ap()
        x1_table = nc.dram_tensor("x1_table", (nodes, D), F32, kind="Internal").ap()

        ident = sb("ident", [P, P])
        iota_i = sb("iota_i", [P, P], I32)
        node_row = sb("node_row", [P, P])
        ids_i = sb("ids_i", [P, blocks], I32)
        node_id = sb("node_id", [P, blocks])
        block_base = sb("block_base", [P, blocks])
        w_lr = sb("w_lr", [P, 2 * D])
        w1, w2 = sb("w1", [P, D]), sb("w2", [P, D])
        att = sb("att", [P, D])
        bias, gamma, beta, b2 = (sb(n, [P, D]) for n in ("bias", "gamma", "beta", "b2"))
        b1 = sb("b1", [P, 1])
        eps = sb("eps", [P, 1])
        ends_i = sb("ends_i", [1, 2 * groups], I32)
        bounds = sb("bounds", [1, 2 * groups], I32)

        xr = sb("xr", [P, blocks, D])
        sums = sb("sums", [P, blocks, WC])
        e_self = sb("e_self", [P, blocks, H])

        src_idx = [sb(f"src_idx{s}", [P, T], I32) for s in range(U)]
        rows = [sb(f"rows{s}", [P, T, D]) for s in range(U)]
        dst_near = [sb(f"dst_near{s}", [P, T + 2], I32) for s in range(U)]
        dst_row = [sb(f"dst_row{s}", [P, G + T], I32) for s in range(U)]
        node_of = [sb(f"node_of{s}", [P, G]) for s in range(2)]
        edge_of = [sb(f"edge_of{s}", [P, T, P]) for s in range(2)]
        relu_h = [sb(f"relu_h{s}", [P, T, D]) for s in range(2)]
        prod = sb("prod", [P, T, D])
        wmsg = [sb(f"wmsg{s}", [P, T, WX]) for s in range(2)]
        dst_big, dst_rel = sb("dst_big", [P, T + 2]), sb("dst_rel", [P, T])
        logit, fwd, run = sb("logit", [P, H * T]), sb("fwd", [P, H * T]), sb("run", [P, H * T])
        step_pen = sb("step_pen", [P, H * T + 1])
        pen_first, pen_last, is_last = (sb(n, [P, T]) for n in ("pen_first", "pen_last", "is_last"))
        row_pen = sb("row_pen", [H, 2, P])
        carry_f, carry_b = sb("carry_f", [H, P + 1]), sb("carry_b", [H, P + 1])
        from_f, from_b, top = sb("from_f", [P, H, T]), sb("from_b", [P, H, T]), sb("top", [P, H, T])
        shifted = sb("shifted", [P, H, T + 1])
        r_exp, first_edge = sb("r_exp", [P, H]), sb("first_edge", [P, 1])
        keep, factor = sb("keep", [P, H]), sb("factor", [P, H])

        ph = [pb(f"ph{s}", [P, T, D]) for s in range(2)]
        pT1, pT2 = pb("pT1", [P, 512]), pb("pT2", [P, 512])
        pA = [pb(f"pA{s}", [P, 512]) for s in range(2)]

        def by_head(t):
            return t[:, 0:H * T].rearrange("p (h t) -> p h t", h=H)

        pool_waits, pe_waits, v_waits = (nc.alloc_semaphore(n) for n in ("pool_waits", "pe_waits", "v_waits"))
        sems = {}

        def S(name):
            if name not in sems:
                sems[name] = nc.alloc_semaphore(name)
            return sems[name]

        def end_phase():
            nc.clear_and_free_semaphores(list(sems.values()))
            nc.all_engine_barrier()
            sems.clear()

        x_pair = a["x"].rearrange("(q b p) d -> q p b d", b=2, p=P)
        xl_pair = xl_table.rearrange("(q b p) d -> q p b d", b=2, p=P)
        x1_pair = x1_table.rearrange("(q b p) d -> q p b d", b=2, p=P)
        out_pair = out.rearrange("(q b p) d -> q p b d", b=2, p=P)
        ring_a = [rows[s // 4][:, 2 * (s % 4):2 * (s % 4) + 2, :] for s in range(UP)]
        ring_b = [rows[2 + s // 4][:, 2 * (s % 4):2 * (s % 4) + 2, :] for s in range(UP)]
        ring_c = [edge_of[s // 4][:, 2 * (s % 4):2 * (s % 4) + 2, :] for s in range(UP)]
        node_tmp = [relu_h[s // 4][:, 2 * (s % 4):2 * (s % 4) + 2, :] for s in range(8)]

        def split(t):
            return t[:, :, :].rearrange("p (q b) k -> p q b k", b=2)

        xr_pair, e_self_pair, sums_pair = split(xr), split(e_self), split(sums)

        def two(t):
            return t[:, :].unsqueeze(1).to_broadcast([P, 2, D])

        with nc.Block() as block:
            @block.sync
            def _(sp):
                for t, n in ((w_lr[:, 0:D], "W_l"), (w_lr[:, D:2 * D], "W_r"), (w1[:, :], "W1"), (w2[:, :], "W2")):
                    sp.dma_start(t, a[n]).then_inc(S("consts_in"), 16)
                for t, n in ((att, "att"), (bias, "bias"), (gamma, "gamma"), (beta, "beta"), (b2, "b2")):
                    sp.dma_start(t[:, :], a[n].partition_broadcast(P)).then_inc(S("consts_in"), 16)
                sp.dma_start(b1[:, :], a["b1"].rearrange("(p o) -> p o", o=1)).then_inc(S("consts_in"), 16)
                ends = a["dst"][1:1 + groups * G].rearrange("(o g e) -> o g e", o=1, e=G)
                end_of = ends_i[:, :].rearrange("o (g k) -> o g k", k=2)
                with nc.allow_non_contiguous_dma(reason="one number of each group"):
                    sp.dma_start(end_of[:, :, 0:1], ends[:, :, 0:1]).then_inc(S("ends_in"), 16)
                    sp.dma_start(end_of[:, :, 1:2], ends[:, :, G - 1:G]).then_inc(S("ends_in"), 16)
                with sp.Fori(0, pairs // UP) as j:
                    for s in range(UP):
                        sp.wait_ge(S("x_taken"), j * UP + (s + 1))
                        sp.dma_start(ring_a[s], x_pair[j * UP + s]).then_inc(S(f"x_in{s}"), 16)

            @block.gpsimd
            def _(pool):
                pool.memset(ident[:, :], 0.0).then_inc(S("ident0"), 1)
                pool.wait_ge(S("ident0"), 1)
                pool.affine_select(out=ident[:, :], in_=ident[:, :], compare_op=ALU.not_equal, fill=1.0,
                                   base=0, pattern=[[-1, P]], channel_multiplier=1).then_inc(S("ident_ready"), 1)
                pool.iota(iota_i[:, :], pattern=[[1, P]], base=0, channel_multiplier=0).then_inc(S("iota_ready"), 1)
                pool.iota(ids_i[:, :], pattern=[[P, blocks]], base=0, channel_multiplier=1)\
                    .then_inc(S("iota_ready"), 1)

            @block.tensor
            def _(pe):
                pe.sem_inc(S("x_taken"), UP)
                pe.wait_ge(S("ident_ready"), 1)
                pe.wait_ge(S("consts_in"), 160)
                with pe.Fori(0, pairs // UP) as j:
                    for s in range(UP):
                        back = 1 if s == 0 else 0
                        pT = (pT1, pT2)[s % 2]
                        pe.wait_ge(S(f"x_in{s}"), j * 16 + 16)
                        pe.wait_ge(S("xT_ready"), j * UP + (s + 1 + back))
                        for b in range(2):
                            ins = pe.transpose(pT[:, b * P:(b + 1) * P], ring_a[s][:, b, :], ident[:, :])
                        ins.then_inc(S("x_taken"), 1)
                        pe.wait_ge(S("xT_ready"), j * UP + (s + 3))
                        pe.wait_ge(S("lr_taken"), j * UP + (s + 1 + back))
                        for b in range(2):
                            ins = pe.matmul(pA[s % 2][:, b * 2 * D:(b + 1) * 2 * D], ring_b[s][:, b, :], w_lr[:, :],
                                            start=True, stop=True)
                        ins.then_inc(S("lr_ready"), 1)

            @block.scalar
            def _(act):
                act.sem_inc(S("xT_ready"), 2)
                with act.Fori(0, pairs // UP) as j:
                    for s in range(UP):
                        pT = (pT1, pT2)[s % 2]
                        act.wait_ge(S("x_taken"), j * UP + (s + 1 + UP))
                        act.activation(ring_b[s], pT[:, 0:2 * P].rearrange("p (b n) -> p b n", b=2), ACT.Copy)\
                           .then_inc(S("xT_ready"), 1)
                        act.wait_ge(S("lr_ready"), j * UP + (s + 1))
                        lr = pA[s % 2][:, :].rearrange("p (b k) -> p b k", b=2)
                        act.activation(ring_c[s], lr[:, :, 0:D], ACT.Copy).then_inc(S("xl_ready"), 1)
                        act.wait_ge(S("xl_ready"), j * UP + (s + 1))
                        act.dma_start(xl_pair[j * UP + s], ring_c[s]).then_inc(S(f"xl_out{s}"), 16)
                    for s in range(UP):
                        act.wait_ge(S(f"xl_out{s}"), j * 16 + 16)

            @block.vector
            def _(v):
                done = 0

                def link(ins):
                    nonlocal done
                    done += 1
                    ins.then_inc(S("node_chain"), 1)
                    v.wait_ge(S("node_chain"), done)

                v.sem_inc(S("lr_taken"), 2)
                v.memset(eps[:, :], EPS)
                v.memset(sums[:, :, :], 0.0)
                v.memset(step_pen[:, :], -BIG)
                for s in range(2):
                    v.memset(wmsg[s][:, :, :], 0.0)
                v.memset(carry_f[:, :], -BIG)
                v.memset(carry_b[:, :], -BIG)
                v.wait_ge(S("iota_ready"), 2)
                v.tensor_copy(node_row[:, :], iota_i[:, :])
                link(v.tensor_copy(node_id[:, :], ids_i[:, :]))
                v.tensor_scalar(block_base[:, :], node_id[:, :], node_id[:, 0:1], None, ALU.subtract)
                link(v.tensor_scalar(first_edge[:, :], node_id[:, 0:1], 0.0, None, ALU.is_equal))
                for s in range(2):
                    v.tensor_copy(wmsg[s][:, 0, WC + H:WX], first_edge[:, 0:1].to_broadcast([P, H]))
                v.wait_ge(S("ends_in"), 32)
                link(v.tensor_scalar(bounds[:, :], ends_i[:, :], 7, None, ALU.arith_shift_right))
                v.wait_ge(S("consts_in"), 160)
                h_self, l_self, m_self = node_tmp[0:3]
                with v.Fori(0, pairs // UP) as j:
                    for s in range(UP):
                        k = j * (4 * UP) + (4 * s + done)
                        both = xr_pair[:, j * UP + s]
                        v.wait_ge(S("xl_ready"), j * UP + (s + 1))
                        r = pA[s % 2][:, :].rearrange("p (b k) -> p b k", b=2)[:, :, D:2 * D]
                        v.tensor_copy(both, r)
                        v.tensor_tensor(h_self, ring_c[s], r, ALU.add).then_inc(S("node_chain"), 1)
                        v.wait_ge(S("node_chain"), k + 1)
                        v.sem_inc(S("lr_taken"), 1)
                        v.scalar_tensor_tensor(l_self, h_self, GAT_SLOPE, h_self, ALU.mult, ALU.max)\
                         .then_inc(S("node_chain"), 1)
                        v.wait_ge(S("node_chain"), k + 2)
                        v.tensor_tensor(m_self, l_self, two(att), ALU.mult).then_inc(S("node_chain"), 1)
                        v.wait_ge(S("node_chain"), k + 3)
                        v.tensor_reduce(e_self_pair[:, j * UP + s], m_self.rearrange("p b (h c) -> p b h c", h=H),
                                        AX.X, ALU.add).then_inc(S("node_chain"), 1)
                        v.wait_ge(S("node_chain"), k + 4)

        end_phase()

        def load_group(sp, g, layer, row):
            s = g.c % U
            sp.wait_ge(S(f"rows_free{layer}{s}"), g.use(1, 1))
            sp.dma_start(src_idx[s][:, :], bass.AP(a["src"].tensor, g.times(G), [[T, P], [1, T]]))\
              .then_inc(S(f"src_in{layer}{s}"), 16)
            sp.wait_ge(S(f"sums_made{layer}"), g.times(1, 1))
            sp.dma_start(dst_near[s][:, :], bass.AP(a["dst"].tensor, g.times(G), [[T, P], [1, T + 2]]))\
              .then_inc(S(f"near_in{layer}{s}"), 16)
            row(g).then_inc(S(f"row_in{layer}{s}"), 16)

        def gather(pool, table, layer):
            with pool.Fori(0, groups // U) as j:
                for s in range(U):
                    wait_alone(pool, pool_waits, S(f"src_in{layer}{s}"), j * 16 + 16)
                    for t in range(T):
                        pool.indirect_dma_start(rows[s][:, t, :], None, table[:, :],
                                                bass.IndirectOffsetOnAxis(ap=src_idx[s][:, t:t + 1], axis=0))\
                            .then_inc(S(f"gathered{layer}{s}"), 16)

        with nc.Block() as block:
            @block.sync
            def _(sp):
                def dst_row_load(g):
                    return sp.dma_start(dst_row[g.c % U][:, 0:G + 2],
                                        bass.AP(a["dst"].tensor, g.times(G), [[0, P], [1, G + 2]]))

                with sp.Fori(0, groups // U) as j:
                    for s in range(U):
                        load_group(sp, Group(j, s), 0, dst_row_load)

            @block.gpsimd
            def _(pool):
                gather(pool, xl_table, 0)

            @block.tensor
            def _(pe):
                block_r, n_h, n_sum = (pe.alloc_register(n) for n in ("pe_block", "pe_n_h", "pe_n_sum"))
                pe.reg_mov(n_h, 0)
                pe.reg_mov(n_sum, 0)
                blk = lambda r: pe.snap(r, min_val=0, max_val=blocks - 1)
                pe.sem_inc(S("node_of_used1"), 1)

                def hidden(g, ends):
                    s, s2 = g.c % U, g.c % 2
                    pe.wait_ge(S(f"gathered0{s}"), g.use(16 * T, 16 * T))
                    if g.at_least(2):
                        pe.wait_ge(S("h_taken"), g.times(1, -1))
                    for k in range(0, T, 4):
                        pe.matmul(ph[s2][:, k:k + 4, :], ident[:, :], rows[s][:, k:k + 4, :], start=True, stop=False)

                    def further():
                        pe.reg_add(n_h, n_h, 1)
                        pe.wait_ge(S("node_of_made1"), pe.snap(n_h, min_val=1, max_val=1 << 20))
                        for t in range(T):
                            ins = pe.matmul(ph[s2][:, t, :], node_of[1][:, t::T], xr[:, blk(block_r), :],
                                            start=False, stop=False)
                        ins.then_inc(S("node_of_used1"), 1)

                    further_visits(pe, block_r, ends, further)
                    pe.wait_ge(S("node_of_made0"), g.times(1, 1))
                    for t in range(T):
                        ins = pe.matmul(ph[s2][:, t, :], node_of[0][:, t::T], xr[:, blk(ends[0]), :],
                                        start=False, stop=(t % 4 == 3))
                    ins.then_inc(S("h_ready"), 1)

                def sum_up(g, ends):
                    w = wmsg[g.c % 2]

                    def visit(k):
                        for t in range(T):
                            ins = pe.matmul(pA[k][:, 0:WX], edge_of[k][:, t, :], w[:, t, :],
                                            start=(t == 0), stop=(t == T - 1))
                        ins.then_inc(S(f"summed{k}"), 1)

                    def further():
                        pe.reg_add(n_sum, n_sum, 1)
                        pe.wait_ge(S("edge_of_made1"), pe.snap(n_sum, min_val=1, max_val=1 << 20))
                        visit(1)

                    pe.wait_ge(S("edge_of_made0"), g.times(1, 1))
                    visit(0)
                    further_visits(pe, block_r, ends, further)

                def step(g, near):
                    if not g.at_least(1):
                        hidden(g, near(g))
                    if not (g.j is None and g.c + 1 >= groups):
                        hidden(g + 1, near(g + 1))
                    if not (g.j is None and g.c >= groups):
                        pe.wait_ge(S("run_ready"), g.times(1, 1))
                        run_h = by_head(run)
                        pe.transpose(pT1[0:H, 0:P], run_h[:, :, T - 1], ident[:, :])
                        pe.transpose(pT1[0:H, P:2 * P], run_h[:, :, 0], ident[:, :]).then_inc(S("ends_across"), 1)
                        wait_alone(pe, pe_waits, S("carry_ready"), g.times(1, 1))
                        pe.transpose(pT2[:, 0:H], carry_f[:, 0:P], ident[0:H, 0:H])
                        pe.transpose(pT2[:, H:2 * H], carry_b[:, 1:P + 1], ident[0:H, 0:H])\
                          .then_inc(S("carry_back"), 1)
                    if g.at_least(1):
                        sum_up(g + -1, near(g + -1))

                sweep(pe, groups, step, bounds)

            @block.scalar
            def _(act):
                def relu(g):
                    act.wait_ge(S("h_ready"), g.times(1, 1))
                    act.activation(relu_h[g.c % 2][:, :, :], ph[g.c % 2][:, :, :], ACT.Relu, scale=1.0 - GAT_SLOPE)\
                       .then_inc(S("relu_ready"), 1)

                def step(g, _):
                    if not g.at_least(1):
                        relu(g)
                    if not (g.j is None and g.c + 1 >= groups):
                        relu(g + 1)
                    if not (g.j is None and g.c >= groups):
                        act.wait_ge(S("shifted_ready"), g.times(1, 1))
                        heads = wmsg[g.c % 2][:, :, 0:H * HC].rearrange("p t (h k) -> p t h k", k=HC)
                        act.activation(heads[:, :, :, C], shifted[:, :, 0:T].rearrange("p h t -> p t h"), ACT.Exp)
                        act.activation(r_exp[:, :], shifted[:, :, T], ACT.Exp).then_inc(S("weights_ready"), 1)

                sweep(act, groups, step)

            @block.vector
            def _(v):
                block_r, n_h, n_sum, n_vis = (v.alloc_register(n) for n in ("v_block", "v_n_h", "v_n_sum", "v_n_vis"))
                for r in (n_h, n_sum, n_vis):
                    v.reg_mov(r, 0)
                blk = lambda r: v.snap(r, min_val=0, max_val=blocks - 1)
                for s in range(U):
                    v.sem_inc(S(f"rows_free0{s}"), 1)
                v.sem_inc(S("sums_made0"), U)
                soft, tail = Chain(v, S("soft_chain")), Chain(v, S("tail_chain"))

                def node_one_hot(g, ends):
                    ids = dst_row[g.c % U][:, 1:1 + G]
                    v.wait_ge(S(f"row_in0{g.c % U}"), g.use(16, 16))
                    if g.at_least(1):
                        v.wait_ge(S("h_ready"), g.times(1, 0))
                    v.tensor_scalar(node_of[0][:, :], ids, node_id[:, bass.ds(blk(ends[0]), 1)], None, ALU.is_equal)\
                     .then_inc(S("node_of_made0"), 1)

                    def further():
                        v.reg_add(n_h, n_h, 1)
                        v.wait_ge(S("node_of_used1"), v.snap(n_h, min_val=1, max_val=1 << 20))
                        v.tensor_scalar(node_of[1][:, :], ids, node_id[:, bass.ds(blk(block_r), 1)], None,
                                        ALU.is_equal).then_inc(S("node_of_made1"), 1)

                    further_visits(v, block_r, ends, further)

                def logits(g):
                    s, s2 = g.c % U, g.c % 2
                    soft.at(g.times(SOFT_LINKS))
                    v.wait_ge(S(f"near_in0{s}"), g.use(16, 16))
                    soft.link(v.tensor_scalar(dst_big[:, :], dst_near[s][:, :], BIG, None, ALU.mult))
                    v.tensor_tensor(by_head(step_pen)[:, :, 1:T], dst_big[:, 1:T].unsqueeze(1).to_broadcast([P, H, T - 1]),
                                    dst_big[:, 2:T + 1].unsqueeze(1).to_broadcast([P, H, T - 1]), ALU.subtract)
                    v.tensor_scalar(pen_first[:, :], dst_big[:, 1:T + 1], dst_big[:, 0:1], -1.0,
                                    ALU.subtract, ALU.mult)
                    v.tensor_scalar(pen_last[:, :], dst_big[:, 1:T + 1], dst_big[:, T + 1:T + 2], None, ALU.subtract)
                    v.tensor_tensor(is_last[:, :], dst_big[:, 1:T + 1], dst_big[:, 2:T + 2], ALU.not_equal)
                    ahead = dst_row[s][0:H, 0:G].rearrange("h (p e) -> h e p", e=T)[:, 0:2, :]
                    behind = dst_row[s][0:H, T:G + T].rearrange("h (p e) -> h e p", e=T)[:, 0:2, :]
                    soft.link(v.tensor_tensor(row_pen[:, :, :], ahead, behind, ALU.subtract))
                    v.tensor_scalar(row_pen[:, :, :], row_pen[:, :, :], BIG, None, ALU.mult)
                    v.wait_ge(S("relu_ready"), g.times(1, 1))
                    v.scalar_tensor_tensor(prod[:, :, :], ph[s2][:, :, :], GAT_SLOPE, relu_h[s2][:, :, :],
                                           ALU.mult, ALU.add).then_inc(S("h_taken"), 1)
                    v.wait_ge(S("h_taken"), g.times(1, 1))
                    soft.link(v.tensor_tensor(prod[:, :, :], prod[:, :, :], att[:, :].unsqueeze(1).to_broadcast([P, T, D]),
                                              ALU.mult))
                    soft.link(v.tensor_reduce(by_head(logit).rearrange("p h t -> p t h"),
                                              prod[:, :, :].rearrange("p t (h c) -> p t h c", h=H), AX.X, ALU.add))
                    soft.link(v.tensor_tensor_scan(fwd[:, :], step_pen[:, 0:H * T], logit[:, :], -BIG, ALU.add, ALU.max))
                    v.tensor_tensor_scan(run[:, ::-1], step_pen[:, :0:-1], fwd[:, ::-1], -BIG,
                                         ALU.add, ALU.max).then_inc(S("run_ready"), 1)

                def weigh(g):
                    s, w = g.c % U, wmsg[g.c % 2]
                    heads = w[:, :, 0:H * HC].rearrange("p t (h k) -> p t h k", k=HC)
                    v.wait_ge(S("weights_ready"), g.times(1, 1))
                    v.tensor_tensor(heads[:, :, :, 0:C], rows[s][:, :, :].rearrange("p t (h c) -> p t h c", h=H),
                                    heads[:, :, :, C:HC].to_broadcast([P, T, H, C]), ALU.mult)\
                     .then_inc(S(f"rows_free0{s}"), 1)
                    v.tensor_scalar(w[:, 0, WC:WC + H], r_exp[:, :], first_edge[:, 0:1], None, ALU.mult)

                def across(g):
                    v.wait_ge(S("ends_across"), g.times(1, 1))
                    v.wait_ge(S("run_ready"), g.times(1, 1))
                    soft.link(v.tensor_copy(carry_f[:, 0:1], carry_f[:, P:P + 1]))
                    v.tensor_tensor_scan(carry_f[:, 1:P + 1], row_pen[:, 0, :], pT1[0:H, 0:P], carry_f[:, 0:1],
                                         ALU.add, ALU.max)
                    v.tensor_tensor_scan(carry_b[:, P - 1::-1], row_pen[:, 1, ::-1], pT1[0:H, 2 * P - 1:P - 1:-1],
                                         -BIG, ALU.add, ALU.max).then_inc(S("carry_ready"), 1)

                def edge_one_hot(g, k, b):
                    s = g.c % U
                    v.tensor_scalar(dst_rel[:, :], dst_near[s][:, 1:T + 1], block_base[:, bass.ds(blk(b), 1)], None,
                                    ALU.subtract).then_inc(S("visit_chain"), 1)
                    v.wait_ge(S("visit_chain"), v.snap(n_vis, min_val=0, max_val=1 << 20) + 1)
                    v.tensor_tensor(edge_of[k][:, :, :], dst_rel[:, :].unsqueeze(2).to_broadcast([P, T, P]),
                                    node_row[:, :].unsqueeze(1).to_broadcast([P, T, P]), ALU.is_equal)\
                     .then_inc(S(f"edge_of_made{k}"), 1)

                def shift(g):
                    w = wmsg[g.c % 2]
                    v.wait_ge(S("carry_back"), g.times(1, 1))
                    v.tensor_tensor(from_f[:, :, :], pT2[:, 0:H].unsqueeze(2).to_broadcast([P, H, T]),
                                    pen_first[:, :].unsqueeze(1).to_broadcast([P, H, T]), ALU.add)
                    soft.link(v.tensor_tensor(from_b[:, :, :], pT2[:, H:2 * H].unsqueeze(2).to_broadcast([P, H, T]),
                                              pen_last[:, :].unsqueeze(1).to_broadcast([P, H, T]), ALU.add))
                    soft.link(v.tensor_tensor(top[:, :, :], from_f[:, :, :], by_head(run), ALU.max))
                    soft.link(v.tensor_tensor(top[:, :, :], top[:, :, :], from_b[:, :, :], ALU.max))
                    v.tensor_tensor(w[:, :, H * HC:WC], top[:, :, :].rearrange("p h t -> p t h"),
                                    is_last[:, :].unsqueeze(2).to_broadcast([P, T, H]), ALU.mult)
                    v.tensor_tensor(shifted[:, :, T], from_f[:, :, 0], top[:, :, 0], ALU.subtract)
                    v.tensor_tensor(shifted[:, :, 0:T], by_head(logit), top[:, :, :], ALU.subtract)\
                     .then_inc(S("shifted_ready"), 1)
                    wait_alone(v, v_waits, S("shifted_ready"), g.times(1, 1))
                    assert soft.n == SOFT_LINKS

                def add_sums(k, b):
                    vis = v.snap(n_vis, min_val=0, max_val=1 << 20)
                    v.tensor_scalar(keep[:, :], pA[k][:, WC + H:WX], -1.0, 1.0, ALU.mult, ALU.add)\
                     .then_inc(S("visit_chain"), 1)
                    v.wait_ge(S("visit_chain"), vis + 2)
                    v.tensor_tensor(factor[:, :], pA[k][:, WC:WC + H], keep[:, :], ALU.add).then_inc(S("visit_chain"), 1)
                    v.wait_ge(S("visit_chain"), vis + 3)
                    old = sums[:, blk(b), 0:H * HC].rearrange("p (h k) -> p h k", k=HC)
                    v.tensor_tensor(old, old, factor[:, :].unsqueeze(2).to_broadcast([P, H, HC]), ALU.mult)\
                     .then_inc(S("visit_chain"), 1)
                    v.wait_ge(S("visit_chain"), vis + 4)
                    v.tensor_tensor(sums[:, blk(b), :], sums[:, blk(b), :], pA[k][:, 0:WC], ALU.add)\
                     .then_inc(S("visit_chain"), 1)
                    v.wait_ge(S("visit_chain"), vis + 5)
                    v.reg_add(n_vis, n_vis, 5)

                def step(g, near):
                    last = g + -1
                    more = not (g.j is None and g.c >= groups)
                    if not g.at_least(1):
                        node_one_hot(g, near(g))
                    if not (g.j is None and g.c + 1 >= groups):
                        node_one_hot(g + 1, near(g + 1))
                    if more:
                        logits(g)
                    if g.at_least(1):
                        weigh(last)
                    if more:
                        across(g)
                    if g.at_least(1):
                        edge_one_hot(last, 0, near(last)[0])
                    if more:
                        shift(g)
                    if g.at_least(1):
                        wait_alone(v, v_waits, S("summed0"), last.times(1, 1))
                        add_sums(0, near(last)[0])

                        def further():
                            v.reg_add(n_sum, n_sum, 1)
                            edge_one_hot(last, 1, block_r)
                            wait_alone(v, v_waits, S("summed1"), v.snap(n_sum, min_val=1, max_val=1 << 20))
                            add_sums(1, block_r)

                        further_visits(v, block_r, near(last), further)
                        v.sem_inc(S("sums_made0"), 1)

                sweep(v, groups, step, bounds)

        def node_loop(eng, stages):
            with eng.Fori(0, pairs // UP) as j:
                for s in range(UP + max(lag for _, lag in stages)):
                    for fn, lag in stages:
                        if 0 <= s - lag < UP:
                            fn(j, s - lag)

        stat = [sb(f"stat{s}", [P, 2, 12]) for s in range(UP)]

        def layer_norm(tag, work):
            def stats(v, j, s):
                k = j * UP + (s + 1)
                for b in range(2):
                    ins = v.bn_stats(stat[s][:, b, 0:6], work[s][:, b, :])
                ins.then_inc(S(f"{tag}_stats"), 1)
                wait_alone(v, v_waits, S(f"{tag}_stats"), k)
                for b in range(2):
                    ins = v.bn_aggr(stat[s][:, b, 6:8], stat[s][:, b, 0:6])
                ins.then_inc(S(f"{tag}_var"), 1)

            def root(act, j, s):
                act.wait_ge(S(f"{tag}_var"), j * UP + (s + 1))
                act.activation(stat[s][:, :, 8], stat[s][:, :, 7], ACT.Sqrt, bias=eps[:, 0:1])\
                   .then_inc(S(f"{tag}_std"), 1)

            def scale(v, j, s):
                k = j * UP + (s + 1)
                v.wait_ge(S(f"{tag}_std"), k)
                v.reciprocal(stat[s][:, :, 9], stat[s][:, :, 8]).then_inc(S(f"{tag}_recip"), 1)
                v.wait_ge(S(f"{tag}_recip"), k)
                for b in range(2):
                    ins = v.tensor_scalar(work[s][:, b, :], work[s][:, b, :], stat[s][:, b, 6:7], stat[s][:, b, 9:10],
                                          ALU.subtract, ALU.mult)
                ins.then_inc(S(f"{tag}_normed"), 1)

            return stats, root, scale

        end_phase()

        def heads_of(t):
            return t.rearrange("p b (h c) -> p b h c", h=H)

        node_m = relu_h[0][:, :, :].rearrange("p t d -> p (t d)")[:, 0:blocks * H].rearrange("p (b h) -> p b h", h=H)
        to_exp = prod[:, :, :].rearrange("p t d -> p (t d)")[:, 0:2 * blocks * H]\
            .rearrange("p (k b h) -> p k b h", k=2, h=H)
        x_ring, xl_ring, o_ring = ring_a, ring_b, ring_c
        t_ring = [node_of[s // 4][:, 256 * (s % 4):256 * (s % 4) + 256].rearrange("p (b d) -> p b d", b=2)
                  for s in range(UP)]
        with nc.Block() as block:
            stats_a, root_a, scale_a = layer_norm("na", o_ring)
            stats_b, root_b, scale_b = layer_norm("nb", o_ring)

            @block.sync
            def _(sp):
                with sp.Fori(0, pairs // UP) as j:
                    for s in range(UP):
                        sp.wait_ge(S("node_in_free"), j * UP + (s + 1))
                        sp.dma_start(x_ring[s], x_pair[j * UP + s]).then_inc(S(f"x_again{s}"), 16)
                        sp.dma_start(xl_ring[s], xl_pair[j * UP + s]).then_inc(S(f"xl_again{s}"), 16)

            @block.gpsimd
            def _(pool):
                pool.sem_inc(S("node_in_free"), UP)
                pool.memset(xr[:, :, :], 0.0)
                pool.wait_ge(S("merged"), 1)

                def selfs(j, s):
                    k = j * UP + (s + 1)
                    pool.wait_ge(S(f"xl_again{s}"), j * 16 + 16)
                    pool.wait_ge(S(f"x_again{s}"), j * 16 + 16)
                    pool.wait_ge(S("t_free"), k)
                    pool.tensor_tensor(heads_of(t_ring[s]), heads_of(xl_ring[s]),
                                       e_self_pair[:, j * UP + s].unsqueeze(3).to_broadcast([P, 2, H, C]), ALU.mult)\
                        .then_inc(S("t_made"), 1)
                    pool.wait_ge(S("t_made"), j * (2 * UP) + (2 * s + 1))
                    pool.tensor_tensor(xl_ring[s], x_ring[s], two(bias), ALU.add).then_inc(S("t_made"), 1)

                def affine(j, s):
                    k = j * UP + (s + 1)
                    pool.wait_ge(S("na_normed"), k)
                    for n, (t, op) in enumerate(((two(gamma), ALU.mult), (two(beta), ALU.add), (x_ring[s], ALU.add))):
                        pool.tensor_tensor(o_ring[s], o_ring[s], t, op).then_inc(S("affine"), 1)
                        pool.wait_ge(S("affine"), j * (3 * UP) + (3 * s + n + 1))
                    pool.sem_inc(S("node_in_free"), 1)

                node_loop(pool, [(selfs, 0), (affine, 1)])

            @block.scalar
            def _(act):
                act.wait_ge(S("merge_in"), 1)
                act.activation(to_exp, to_exp, ACT.Exp).then_inc(S("merge_exp"), 1)

                def store(j, s):
                    act.wait_ge(S("nb_normed"), j * UP + (s + 1))
                    act.dma_start(x1_pair[j * UP + s], o_ring[s]).then_inc(S(f"x1_out{s}"), 16)
                    if s == UP - 1:
                        for n in range(UP):
                            act.wait_ge(S(f"x1_out{n}"), j * 16 + 16)
                        act.sem_inc(S("x1_free"), UP)

                node_loop(act, [(lambda j, s: root_a(act, j, s), 0), (lambda j, s: root_b(act, j, s), 2), (store, 3)])

            @block.vector
            def _(v):
                n = 0

                def link(ins):
                    nonlocal n
                    n += 1
                    ins.then_inc(S("merge_chain"), 1)
                    v.wait_ge(S("merge_chain"), n)

                v.sem_inc(S("t_free"), UP)
                v.sem_inc(S("x1_free"), UP)
                den = sums[:, :, 0:H * HC].rearrange("p b (h k) -> p b h k", k=HC)[:, :, :, C]
                peak = sums[:, :, H * HC:WC]
                link(v.tensor_scalar(node_m, den, 0.0, -BIG, ALU.is_le, ALU.mult))
                link(v.tensor_tensor(peak, peak, node_m, ALU.add))
                link(v.tensor_tensor(node_m, peak, e_self[:, :, :], ALU.max))
                v.tensor_tensor(to_exp[:, 0], peak, node_m, ALU.subtract)
                v.tensor_tensor(to_exp[:, 1], e_self[:, :, :], node_m, ALU.subtract).then_inc(S("merge_in"), 1)
                v.wait_ge(S("merge_exp"), 1)
                link(v.tensor_tensor(node_m, den, to_exp[:, 0], ALU.mult))
                link(v.tensor_tensor(node_m, node_m, to_exp[:, 1], ALU.add))
                link(v.reciprocal(node_m, node_m))
                v.tensor_tensor(peak, to_exp[:, 0], node_m, ALU.mult)
                v.tensor_tensor(e_self[:, :, :], to_exp[:, 1], node_m, ALU.mult).then_inc(S("merged"), 1)
                v.wait_ge(S("merged"), 1)

                def combine(j, s):
                    q = j * UP + s
                    k = j * (3 * UP) + 3 * s
                    num = sums_pair[:, q, :, 0:H * HC].rearrange("p b (h k) -> p b h k", k=HC)[:, :, :, 0:C]
                    scale = sums_pair[:, q, :, H * HC:WC].unsqueeze(3).to_broadcast([P, 2, H, C])
                    v.wait_ge(S("x1_free"), j * UP + UP)
                    v.tensor_tensor(heads_of(o_ring[s]), num, scale, ALU.mult).then_inc(S("comb"), 1)
                    v.wait_ge(S("t_made"), j * (2 * UP) + (2 * s + 2))
                    v.wait_ge(S("comb"), k + 1)
                    v.tensor_tensor(o_ring[s], o_ring[s], t_ring[s], ALU.add).then_inc(S("comb"), 1)
                    v.wait_ge(S("comb"), k + 2)
                    v.tensor_tensor(o_ring[s], o_ring[s], xl_ring[s], ALU.add).then_inc(S("comb"), 1)
                    v.wait_ge(S("comb"), k + 3)
                    v.sem_inc(S("t_free"), 1)
                    stats_a(v, j, s)

                def second(j, s):
                    v.wait_ge(S("affine"), j * (3 * UP) + (3 * s + 3))
                    stats_b(v, j, s)

                node_loop(v, [(combine, 0), (lambda j, s: scale_a(v, j, s), 1), (second, 2),
                              (lambda j, s: scale_b(v, j, s), 3)])

        end_phase()

        neigh = xr
        edge_buf = [edge_of[0], edge_of[1], node_of[0][:, :].rearrange("p (t n) -> p t n", t=T)]
        attr = [dst_row[s][:, 0:G].bitcast(F32).rearrange("p (t d) -> p t d", t=T) for s in range(U)]
        msg = relu_h
        banks = [pA[0], pA[1], pT1]
        with nc.Block() as block:
            @block.sync
            def _(sp):
                def attr_load(g, parts=P):
                    src = bass.AP(a["edge_attr"].tensor, g.times(G * D), [[T * D, parts], [1, T * D]])
                    return sp.dma_start(attr[g.c % U][0:parts].rearrange("p t d -> p (t d)"), src)

                with sp.Fori(0, groups // U - 1) as j:
                    for s in range(U):
                        load_group(sp, Group(j, s), 1, attr_load)
                for n in range(groups - U, groups):
                    parts = min(P, -(-(edges - n * G) // T))
                    load_group(sp, Group(None, n), 1, lambda g: attr_load(g, parts))

            @block.gpsimd
            def _(pool):
                gather(pool, x1_table, 1)

            @block.tensor
            def _(pe):
                block_r, n_sum = pe.alloc_register("pe1_block"), pe.alloc_register("pe1_n_sum")
                pe.reg_mov(n_sum, 0)

                def visit(k, m):
                    for t in range(T):
                        ins = pe.matmul(banks[k][:, 0:D], edge_buf[k][:, t, :], m[:, t, :],
                                        start=(t == 0), stop=(t == T - 1))
                    return ins

                def step(g, near):
                    if g.j is None and g.c >= groups:
                        return

                    def further():
                        pe.reg_add(n_sum, n_sum, 1)
                        pe.wait_ge(S("again_made"), pe.snap(n_sum, min_val=1, max_val=1 << 20))
                        visit(2, msg[g.c % 2]).then_inc(S("again_summed"), 1)

                    pe.wait_ge(S("msg_made"), g.times(1, 1))
                    visit(g.c % 2, msg[g.c % 2]).then_inc(S("msg_summed"), 1)
                    further_visits(pe, block_r, near(g), further)

                sweep(pe, groups, step, bounds, 1)

            @block.vector
            def _(v):
                block_r, n_sum, n_vis = (v.alloc_register(n) for n in ("v1_block", "v1_n_sum", "v1_n_vis"))
                v.reg_mov(n_sum, 0)
                v.reg_mov(n_vis, 0)
                blk = lambda r: v.snap(r, min_val=0, max_val=blocks - 1)
                for s in range(U):
                    v.sem_inc(S(f"rows_free1{s}"), 1)
                v.sem_inc(S("sums_made1"), U)

                def one_hot(g, k, b):
                    v.tensor_scalar(dst_rel[:, :], dst_near[g.c % U][:, 1:T + 1], block_base[:, bass.ds(blk(b), 1)], None,
                                    ALU.subtract).then_inc(S("visit1_chain"), 1)
                    v.wait_ge(S("visit1_chain"), v.snap(n_vis, min_val=0, max_val=1 << 20) + 1)
                    v.reg_add(n_vis, n_vis, 1)
                    return v.tensor_tensor(edge_buf[k][:, :, :], dst_rel[:, :].unsqueeze(2).to_broadcast([P, T, P]),
                                           node_row[:, :].unsqueeze(1).to_broadcast([P, T, P]), ALU.is_equal)

                def add(k, b):
                    v.tensor_tensor(neigh[:, blk(b), :], neigh[:, blk(b), :], banks[k][:, 0:D], ALU.add)\
                     .then_inc(S("visit1_chain"), 1)
                    v.wait_ge(S("visit1_chain"), v.snap(n_vis, min_val=0, max_val=1 << 20) + 1)
                    v.reg_add(n_vis, n_vis, 1)

                def step(g, near):
                    if not (g.j is None and g.c >= groups):
                        s = g.c % U
                        v.wait_ge(S(f"near_in1{s}"), g.use(16, 16))
                        one_hot(g, g.c % 2, near(g)[0])
                        v.wait_ge(S(f"gathered1{s}"), g.use(16 * T, 16 * T))
                        v.wait_ge(S(f"row_in1{s}"), g.use(16, 16))
                        v.tensor_tensor(msg[g.c % 2][:, :, :], rows[s][:, :, :], attr[s][:, :, :], ALU.add)\
                         .then_inc(S("msg_made"), 1)
                        v.wait_ge(S("msg_made"), g.times(1, 1))
                        v.sem_inc(S(f"rows_free1{s}"), 1)
                    if g.at_least(1):
                        last = g + -1
                        v.wait_ge(S("msg_summed"), last.times(1, 1))
                        add(last.c % 2, near(last)[0])

                        def further():
                            v.reg_add(n_sum, n_sum, 1)
                            one_hot(last, 2, block_r).then_inc(S("again_made"), 1)
                            v.wait_ge(S("again_summed"), v.snap(n_sum, min_val=1, max_val=1 << 20))
                            add(2, block_r)

                        further_visits(v, block_r, near(last), further)
                        v.sem_inc(S("sums_made1"), 1)

                sweep(v, groups, step, bounds, 1)

        end_phase()

        x1_ring, h_ring, mlp_ring = ring_a, ring_b, ring_c
        hT_ring = t_ring
        with nc.Block() as block:
            stats_c, root_c, scale_c = layer_norm("nc", mlp_ring)

            @block.sync
            def _(sp):
                with sp.Fori(0, pairs // UP) as j:
                    for s in range(UP):
                        sp.wait_ge(S("x1_in_free"), j * UP + (s + 1))
                        sp.dma_start(x1_ring[s], x1_pair[j * UP + s]).then_inc(S(f"x1_in{s}"), 16)

            @block.gpsimd
            def _(pool):
                def residual(j, s):
                    pool.wait_ge(S("mlp_in"), j * UP + (s + 1))
                    pool.tensor_tensor(x1_ring[s], x1_ring[s], two(b2), ALU.add).then_inc(S("res_made"), 1)

                node_loop(pool, [(residual, 0)])

            @block.tensor
            def _(pe):
                def up(j, s):
                    k = j * UP + (s + 1)
                    pe.wait_ge(S("mlp_in"), k)
                    pe.wait_ge(S("hT_ready"), k)
                    for b in range(2):
                        ins = pe.transpose(pT1[:, b * P:(b + 1) * P], h_ring[s][:, b, :], ident[:, :])
                    ins.then_inc(S("h_across"), 1)
                    pe.wait_ge(S("hT_ready"), k + 1)
                    pe.wait_ge(S("z_ready"), k)
                    pe.matmul(pT2[:, 0:2 * P], w1[:, :], hT_ring[s].rearrange("p b n -> p (b n)"), start=True, stop=True)\
                      .then_inc(S("z_made"), 1)

                def down(j, s):
                    k = j * UP + (s + 1)
                    pe.wait_ge(S("act_made"), k)
                    pe.wait_ge(S("mlp_taken"), k)
                    for b in range(2):
                        ins = pe.matmul(pA[0][:, b * D:(b + 1) * D], h_ring[s][:, b, :], w2[:, :], start=True, stop=True)
                    ins.then_inc(S("mlp_ready"), 1)

                node_loop(pe, [(up, 0), (down, 1)])

            @block.scalar
            def _(act):
                act.sem_inc(S("hT_ready"), 1)
                act.sem_inc(S("z_ready"), 1)

                def up(j, s):
                    k = j * UP + (s + 1)
                    act.wait_ge(S("h_across"), k)
                    act.activation(hT_ring[s], pT1[:, 0:2 * P].rearrange("p (b n) -> p b n", b=2), ACT.Copy)\
                       .then_inc(S("hT_ready"), 1)
                    act.wait_ge(S("z_made"), k)
                    act.activation(h_ring[s], pT2[:, 0:2 * P].rearrange("p (b n) -> p b n", b=2), ACT.Identity,
                                   bias=b1[:, 0:1]).then_inc(S("z_ready"), 1)

                def store(j, s):
                    act.wait_ge(S("nc_normed"), j * UP + (s + 1))
                    act.dma_start(out_pair[j * UP + s], mlp_ring[s]).then_inc(S(f"out{s}"), 16)
                    if s == UP - 1:
                        for n in range(UP):
                            act.wait_ge(S(f"out{n}"), j * 16 + 16)
                        act.sem_inc(S("out_free"), UP)

                node_loop(act, [(up, 0), (lambda j, s: root_c(act, j, s), 2), (store, 3)])

            @block.vector
            def _(v):
                v.sem_inc(S("x1_in_free"), UP)
                v.sem_inc(S("mlp_taken"), 1)
                v.sem_inc(S("out_free"), UP)

                def mlp_in(j, s):
                    v.wait_ge(S(f"x1_in{s}"), j * 16 + 16)
                    v.scalar_tensor_tensor(h_ring[s], x1_ring[s], 2.0, split(neigh)[:, j * UP + s], ALU.mult, ALU.add)\
                     .then_inc(S("mlp_in"), 1)

                def leaky(j, s):
                    v.wait_ge(S("z_ready"), j * UP + (s + 2))
                    v.scalar_tensor_tensor(h_ring[s], h_ring[s], MLP_SLOPE, h_ring[s], ALU.mult, ALU.max)\
                     .then_inc(S("act_made"), 1)

                def residual(j, s):
                    k = j * UP + (s + 1)
                    v.wait_ge(S("out_free"), j * UP + UP)
                    v.wait_ge(S("mlp_ready"), k)
                    v.wait_ge(S("res_made"), k)
                    v.tensor_tensor(mlp_ring[s], x1_ring[s], pA[0][:, 0:2 * D].rearrange("p (b d) -> p b d", b=2), ALU.add)\
                     .then_inc(S("res_added"), 1)
                    v.wait_ge(S("res_added"), k)
                    v.sem_inc(S("mlp_taken"), 1)
                    v.sem_inc(S("x1_in_free"), 1)
                    stats_c(v, j, s)

                node_loop(v, [(mlp_in, 0), (leaky, 1), (residual, 2), (lambda j, s: scale_c(v, j, s), 3)])


def kernel(**inputs):
    import numpy as np
    import concourse.bacc as bacc
    from concourse.bass_utils import run_bass_kernel_spmd

    x = np.ascontiguousarray(inputs["x"])
    src, dst = np.asarray(inputs["src"]), np.asarray(inputs["dst"])
    n, edges = x.shape[0], src.shape[0]
    blocks = -(-(n + 1) // (2 * UP * P)) * 2 * UP
    groups = -(-edges // (U * G)) * U
    spare = groups * G - edges
    arrays = {
        "x": np.concatenate([x, np.zeros((blocks * P - n, D), x.dtype)]),
        "src": np.concatenate([src, np.zeros(spare, src.dtype)]),
        "dst": np.concatenate([np.full(1, -1, dst.dtype), dst, np.full(spare, blocks * P - 1, dst.dtype),
                               np.full(1, blocks * P, dst.dtype)]),
        "edge_attr": np.ascontiguousarray(inputs["edge_attr_128"]),
        "att": np.ascontiguousarray(inputs["L0_gnn_att"]).reshape(D),
    }
    for name, of in (("W_l", "L0_gnn_W_l"), ("W_r", "L0_gnn_W_r"), ("bias", "L0_gnn_bias"), ("gamma", "L0_gnn_ln_gamma"),
                     ("beta", "L0_gnn_ln_beta"), ("W1", "L1_gnn_W1"), ("b1", "L1_gnn_b1"), ("W2", "L1_gnn_W2"),
                     ("b2", "L1_gnn_b2")):
        arrays[name] = np.ascontiguousarray(inputs[of])
    nc = bacc.Bacc("TRN2", target_bir_lowering=False, num_devices=1)
    aps = {k: nc.dram_tensor(f"in_{k}", v.shape, mybir.dt.from_np(v.dtype), kind="ExternalInput").ap()
           for k, v in arrays.items()}
    out = nc.dram_tensor("out_x", (blocks * P, D), F32, kind="ExternalOutput").ap()
    build(nc, aps, out, edges, groups, blocks)
    r = run_bass_kernel_spmd(nc, [{f"in_{k}": v for k, v in arrays.items()}], core_ids=[0])
    return r.results[0]["out_x"][0:n]
```

```python
from contextlib import ExitStack

import concourse.bass as bass
from concourse import mybir

F32 = mybir.dt.float32
I32 = mybir.dt.int32
ALU = mybir.AluOpType
ACT = mybir.ActivationFunctionType
AX = mybir.AxisListType

P = 128
D = 128
H = 4
C = D // H
T = 8
G = P * T
U = 4
UP = 7
HC = C + 1
WC = H * HC + H
NA = 56
BIG = 2.0 ** 112
GAT_SLOPE, MLP_SLOPE, EPS = 0.2, 0.01, 1e-5
SOFT_LINKS = 8
PREPARE_LINKS = 3
HIDE_LINKS = 1


class Group:

    def __init__(self, j, c):
        self.j, self.c = j, c

    def __add__(self, n):
        return Group(self.j, self.c + n)

    def times(self, a, b=0):
        return a * self.c + b if self.j is None else self.j * (U * a) + (a * self.c + b)

    def use(self, a, b):
        return a * (self.c // U) + b if self.j is None else self.j * a + (a * (self.c // U) + b)

    def at_least(self, n):
        return self.j is not None or self.c >= n


def sweep(eng, groups, step, ends=None, layer=0):

    def part(tag, j, first, steps, lo, n):
        regs = []
        if ends is not None:
            regs = [eng.alloc_register(f"ends{layer}_{tag}_{k}") for k in range(2 * n)]
            eng.load(regs, ends[0:1, bass.ds(2 * first if j is None else j * (2 * U), 2 * n)])
        for c in steps:
            step(Group(j, c), lambda g: (regs[2 * (g.c - lo)], regs[2 * (g.c - lo) + 1]))

    part("head", None, 0, [0], 0, 2)
    with eng.Fori(0, groups // U - 1) as j:
        part("body", j, 0, range(1, U + 1), 0, U + 2)
    base = groups - U
    part("tail", None, base, range(base + 1, groups + 1), base, U)


def further_windows(eng, n, span, body):
    eng.reg_mov(n, 1)
    with eng.While(lambda: eng.snap(n) <= eng.snap(span[1])):
        body()
        eng.reg_add(n, n, 1)


def further_visits(eng, block, ends, body):
    first, last = ends
    eng.reg_add(block, first, 1)
    with eng.While(lambda: eng.snap(block) <= eng.snap(last)):
        body()
        eng.reg_add(block, block, 1)


def wait_alone(eng, waits, sem, value):
    eng.wait_ge(sem, value)
    eng.sem_inc(waits, 1)


class Chain:

    def __init__(self, eng, sem):
        self.eng, self.sem, self.base, self.n = eng, sem, 0, 0

    def at(self, base, n=0):
        self.base, self.n = base, n

    def mark(self, ins):
        self.n += 1
        ins.then_inc(self.sem, 1)

    def link(self, ins):
        self.mark(ins)
        self.eng.wait_ge(self.sem, self.base + self.n)


def build(nc, a, out, edges, groups, blocks):
    nodes = blocks * P
    pairs = blocks // 2
    assert groups % U == 0 and groups > U and pairs % UP == 0
    assert edges % T == 0 and 0 < groups * G - edges < G
    ctx = ExitStack()
    with ctx:
        def sb(name, shape, dt=F32):
            return ctx.enter_context(nc.sbuf_tensor(name, shape, dt))

        def pb(name, shape):
            return ctx.enter_context(nc.psum_tensor(name, shape, F32))

        xl_table = nc.dram_tensor("xl_table", (nodes, D), F32, kind="Internal").ap()
        xr_table = nc.dram_tensor("xr_table", (nodes + P, D), F32, kind="Internal").ap()
        sums_table = nc.dram_tensor("sums_table", (nodes + P, WC), F32, kind="Internal").ap()
        x1_table = nc.dram_tensor("x1_table", (nodes, D), F32, kind="Internal").ap()

        ident = sb("ident", [P, P])
        iota_i = sb("iota_i", [P, P], I32)
        node_row = sb("node_row", [P, P])
        ids_i = sb("ids_i", [P, blocks], I32)
        node_id = sb("node_id", [P, blocks])
        block_base = sb("block_base", [P, blocks])
        w_lr = sb("w_lr", [P, 2 * D])
        w1, w2 = sb("w1", [P, D]), sb("w2", [P, D])
        att = sb("att", [P, D])
        att_col = sb("att_col", [P, 1])
        att_heads = sb("att_heads", [P, NA])
        first_row = sb("first_row", [1, P])
        bias, gamma, beta, b2 = (sb(n, [P, D]) for n in ("bias", "gamma", "beta", "b2"))
        b1 = sb("b1", [P, 1])
        eps = sb("eps", [P, 1])
        ends_i = sb("ends_i", [1, 2 * groups], I32)
        bounds = sb("bounds", [1, 2 * groups], I32)
        spans = sb("spans", [1, 2 * groups], I32)

        xr = sb("xr", [P, blocks, D])
        sums = sb("sums", [P, blocks, WC])
        e_self = sb("e_self", [P, blocks, H])

        src_idx = [sb(f"src_idx{s}", [P, T], I32) for s in range(U)]
        rows = [sb(f"rows{s}", [P, T, D]) for s in range(U)]
        dst_near = [sb(f"dst_near{s}", [P, T + 2], I32) for s in range(U)]
        dst_row = [sb(f"dst_row{s}", [P, G + T], I32) for s in range(U)]
        xr_win = [sb(f"xr_win{s}", [P, D]) for s in range(U)]
        xr_more = sb("xr_more", [P, D])
        node_of = [sb(f"node_of{s}", [P, G]) for s in range(2)]
        edge_of = [sb(f"edge_of{s}", [P, T, P]) for s in range(2)]
        relu_h = [sb(f"relu_h{s}", [P, T, D]) for s in range(2)]
        prod = sb("prod", [P, T, D])
        wmsg = [sb(f"wmsg{s}", [P, T, WC]) for s in range(2)]
        win = sb("win", [P, WC])
        dst_big, dst_rel = sb("dst_big", [P, T + 2]), sb("dst_rel", [P, T])
        fwd, run = sb("fwd", [P, H * T]), sb("run", [P, H * T])
        step_pen = sb("step_pen", [P, H * T + 1])
        pen_first, pen_last, is_last = (sb(n, [P, T]) for n in ("pen_first", "pen_last", "is_last"))
        row_pen = sb("row_pen", [H, 2, P])
        carry_f, carry_b = sb("carry_f", [H, P + 1]), sb("carry_b", [H, P + 1])
        from_f, from_b, top = sb("from_f", [P, H, T]), sb("from_b", [P, H, T]), sb("top", [P, H, T])
        shifted = sb("shifted", [P, H, T + 1])
        r_exp, first_node = sb("r_exp", [P, H]), sb("first_node", [P, U])
        last_node = sb("last_node", [P, U])
        carried = sb("carried", [1, WC])

        ph = [pb(f"ph{s}", [P, T, D]) for s in range(2)]
        pT1, pT2 = pb("pT1", [P, 512]), pb("pT2", [P, 512])
        pA = [pb(f"pA{s}", [P, 512]) for s in range(2)]

        def by_head(t):
            return t[:, 0:H * T].rearrange("p (h t) -> p h t", h=H)

        node_more = prod[:, :, :].rearrange("p t d -> p (t d)")
        logit_all = pT2[:, 32:32 + T * NA]
        logit = logit_all[:, 0:H * T]
        pick = pA[1][0:1, 256:256 + WC]

        pool_waits, pe_waits, v_waits, sp_waits, act_waits = (
            nc.alloc_semaphore(n) for n in ("pool_waits", "pe_waits", "v_waits", "sp_waits", "act_waits"))
        sems = {}

        def S(name):
            if name not in sems:
                sems[name] = nc.alloc_semaphore(name)
            return sems[name]

        def end_phase():
            nc.clear_and_free_semaphores(list(sems.values()))
            nc.all_engine_barrier()
            sems.clear()

        x_pair = a["x"].rearrange("(q b p) d -> q p b d", b=2, p=P)
        xl_pair = xl_table.rearrange("(q b p) d -> q p b d", b=2, p=P)
        x1_pair = x1_table.rearrange("(q b p) d -> q p b d", b=2, p=P)
        out_pair = out.rearrange("(q b p) d -> q p b d", b=2, p=P)
        xr_blocks = xr_table[0:nodes, :].rearrange("(j b p) d -> j p b d", b=2 * UP, p=P)
        sums_blocks = sums_table[0:nodes, :].rearrange("(j b p) k -> j p b k", b=2 * UP, p=P)
        ring_a = [rows[s // 4][:, 2 * (s % 4):2 * (s % 4) + 2, :] for s in range(UP)]
        ring_b = [rows[2 + s // 4][:, 2 * (s % 4):2 * (s % 4) + 2, :] for s in range(UP)]
        ring_c = [edge_of[s // 4][:, 2 * (s % 4):2 * (s % 4) + 2, :] for s in range(UP)]
        node_tmp = [relu_h[s // 4][:, 2 * (s % 4):2 * (s % 4) + 2, :] for s in range(8)]

        def split(t):
            return t[:, :, :].rearrange("p (q b) k -> p q b k", b=2)

        xr_pair, e_self_pair, sums_pair = split(xr), split(e_self), split(sums)

        def two(t):
            return t[:, :].unsqueeze(1).to_broadcast([P, 2, D])

        with nc.Block() as block:
            @block.sync
            def _(sp):
                for t, n in ((w_lr[:, 0:D], "W_l"), (w_lr[:, D:2 * D], "W_r"), (w1[:, :], "W1"), (w2[:, :], "W2")):
                    sp.dma_start(t, a[n]).then_inc(S("consts_in"), 16)
                sp.dma_start(att_col[:, :], a["att"].rearrange("(p o) -> p o", o=1)).then_inc(S("consts_in"), 16)
                for t, n in ((att, "att"), (bias, "bias"), (gamma, "gamma"), (beta, "beta"), (b2, "b2")):
                    sp.dma_start(t[:, :], a[n].partition_broadcast(P)).then_inc(S("consts_in"), 16)
                sp.dma_start(b1[:, :], a["b1"].rearrange("(p o) -> p o", o=1)).then_inc(S("consts_in"), 16)
                ends = a["dst"][1:1 + groups * G].rearrange("(o g e) -> o g e", o=1, e=G)
                end_of = ends_i[:, :].rearrange("o (g k) -> o g k", k=2)
                with nc.allow_non_contiguous_dma(reason="one number of each group"):
                    sp.dma_start(end_of[:, :, 0:1], ends[:, :, 0:1]).then_inc(S("ends_in"), 16)
                    sp.dma_start(end_of[:, :, 1:2], ends[:, :, G - 1:G]).then_inc(S("ends_in"), 16)
                with sp.Fori(0, pairs // UP) as j:
                    for s in range(UP):
                        sp.wait_ge(S("x_taken"), j * UP + (s + 1))
                        sp.dma_start(ring_a[s], x_pair[j * UP + s]).then_inc(S(f"x_in{s}"), 16)

            @block.gpsimd
            def _(pool):
                pool.memset(ident[:, :], 0.0).then_inc(S("ident0"), 1)
                pool.wait_ge(S("ident0"), 1)
                pool.affine_select(out=ident[:, :], in_=ident[:, :], compare_op=ALU.not_equal, fill=1.0,
                                   base=0, pattern=[[-1, P]], channel_multiplier=1).then_inc(S("ident_ready"), 1)
                pool.iota(iota_i[:, :], pattern=[[1, P]], base=0, channel_multiplier=0).then_inc(S("iota_ready"), 1)
                pool.iota(ids_i[:, :], pattern=[[P, blocks]], base=0, channel_multiplier=1)\
                    .then_inc(S("iota_ready"), 1)

            @block.tensor
            def _(pe):
                pe.sem_inc(S("x_taken"), UP)
                pe.wait_ge(S("ident_ready"), 1)
                pe.wait_ge(S("consts_in"), 176)
                with pe.Fori(0, pairs // UP) as j:
                    for s in range(UP):
                        back = 1 if s == 0 else 0
                        pT = (pT1, pT2)[s % 2]
                        pe.wait_ge(S(f"x_in{s}"), j * 16 + 16)
                        pe.wait_ge(S("xT_ready"), j * UP + (s + 1 + back))
                        for b in range(2):
                            ins = pe.transpose(pT[:, b * P:(b + 1) * P], ring_a[s][:, b, :], ident[:, :])
                        ins.then_inc(S("x_taken"), 1)
                        pe.wait_ge(S("xT_ready"), j * UP + (s + 3))
                        pe.wait_ge(S("lr_taken"), j * UP + (s + 1 + back))
                        for b in range(2):
                            ins = pe.matmul(pA[s % 2][:, b * 2 * D:(b + 1) * 2 * D], ring_b[s][:, b, :], w_lr[:, :],
                                            start=True, stop=True)
                        ins.then_inc(S("lr_ready"), 1)

            @block.scalar
            def _(act):
                act.sem_inc(S("xT_ready"), 2)
                act.wait_ge(S("zeros_ready"), 1)
                act.dma_start(xr_table[nodes:nodes + P, :], win[:, 0:D]).then_inc(S("pad_out"), 16)
                with act.Fori(0, pairs // UP) as j:
                    for s in range(UP):
                        pT = (pT1, pT2)[s % 2]
                        act.wait_ge(S("x_taken"), j * UP + (s + 1 + UP))
                        act.activation(ring_b[s], pT[:, 0:2 * P].rearrange("p (b n) -> p b n", b=2), ACT.Copy)\
                           .then_inc(S("xT_ready"), 1)
                        act.wait_ge(S("lr_ready"), j * UP + (s + 1))
                        lr = pA[s % 2][:, :].rearrange("p (b k) -> p b k", b=2)
                        act.activation(ring_c[s], lr[:, :, 0:D], ACT.Copy).then_inc(S("xl_ready"), 1)
                        act.wait_ge(S("xl_ready"), j * UP + (s + 1))
                        act.dma_start(xl_pair[j * UP + s], ring_c[s]).then_inc(S(f"xl_out{s}"), 16)
                    act.wait_ge(S("xr_ready"), j * UP + UP)
                    act.dma_start(xr_blocks[j], xr[:, bass.ds(j * (2 * UP), 2 * UP), :]).then_inc(S("xr_out"), 16)
                    for s in range(UP):
                        act.wait_ge(S(f"xl_out{s}"), j * 16 + 16)
                act.wait_ge(S("xr_out"), 16 * (pairs // UP))
                act.wait_ge(S("pad_out"), 16)

            @block.vector
            def _(v):
                done = 0

                def link(ins):
                    nonlocal done
                    done += 1
                    ins.then_inc(S("node_chain"), 1)
                    v.wait_ge(S("node_chain"), done)

                v.sem_inc(S("lr_taken"), 2)
                v.memset(eps[:, :], EPS)
                v.memset(step_pen[:, :], -BIG)
                v.memset(win[:, :], 0.0).then_inc(S("zeros_ready"), 1)
                v.memset(carried[:, :], 0.0)
                v.memset(carry_f[:, :], -BIG)
                v.memset(carry_b[:, :], -BIG)
                v.wait_ge(S("iota_ready"), 2)
                v.tensor_copy(node_row[:, :], iota_i[:, :])
                link(v.tensor_copy(node_id[:, :], ids_i[:, :]))
                v.tensor_scalar(block_base[:, :], node_id[:, :], node_id[:, 0:1], None, ALU.subtract)
                link(v.tensor_scalar(first_row[:, :], node_row[0:1, :], 0.0, None, ALU.is_equal))
                v.wait_ge(S("ends_in"), 32)
                v.tensor_scalar(bounds[:, :], ends_i[:, :], 7, None, ALU.arith_shift_right)
                pair_of = [t[:, :].rearrange("o (g k) -> o g k", k=2) for t in (ends_i, spans)]
                link(v.tensor_copy(spans[:, :], ends_i[:, :]))
                link(v.tensor_tensor(pair_of[1][:, :, 1], pair_of[0][:, :, 1], pair_of[0][:, :, 0], ALU.subtract))
                link(v.tensor_scalar(pair_of[1][:, :, 1], pair_of[1][:, :, 1], 7, None, ALU.arith_shift_right))
                v.wait_ge(S("consts_in"), 176)
                link(v.memset(att_heads[:, :], 0.0))
                for h in range(H):
                    link(v.tensor_copy(att_heads[C * h:C * (h + 1), h:h + 1], att_col[C * h:C * (h + 1), :]))
                h_self, l_self, m_self = node_tmp[0:3]
                with v.Fori(0, pairs // UP) as j:
                    for s in range(UP):
                        k = j * (4 * UP) + (4 * s + done)
                        both = xr_pair[:, j * UP + s]
                        v.wait_ge(S("xl_ready"), j * UP + (s + 1))
                        r = pA[s % 2][:, :].rearrange("p (b k) -> p b k", b=2)[:, :, D:2 * D]
                        v.tensor_copy(both, r).then_inc(S("xr_ready"), 1)
                        v.tensor_tensor(h_self, ring_c[s], r, ALU.add).then_inc(S("node_chain"), 1)
                        v.wait_ge(S("node_chain"), k + 1)
                        v.sem_inc(S("lr_taken"), 1)
                        v.scalar_tensor_tensor(l_self, h_self, GAT_SLOPE, h_self, ALU.mult, ALU.max)\
                         .then_inc(S("node_chain"), 1)
                        v.wait_ge(S("node_chain"), k + 2)
                        v.tensor_tensor(m_self, l_self, two(att), ALU.mult).then_inc(S("node_chain"), 1)
                        v.wait_ge(S("node_chain"), k + 3)
                        v.tensor_reduce(e_self_pair[:, j * UP + s], m_self.rearrange("p b (h c) -> p b h c", h=H),
                                        AX.X, ALU.add).then_inc(S("node_chain"), 1)
                        v.wait_ge(S("node_chain"), k + 4)

        end_phase()

        def load_group(sp, g, layer, row):
            s = g.c % U
            sp.wait_ge(S(f"rows_free{layer}{s}"), g.use(1, 1))
            sp.dma_start(src_idx[s][:, :], bass.AP(a["src"].tensor, g.times(G), [[T, P], [1, T]]))\
              .then_inc(S(f"src_in{layer}{s}"), 16)
            sp.wait_ge(S(f"dst_taken{layer}"), g.times(1, 1))
            sp.dma_start(dst_near[s][:, :], bass.AP(a["dst"].tensor, g.times(G), [[T, P], [1, T + 2]]))\
              .then_inc(S(f"near_in{layer}{s}"), 16)
            row(g).then_inc(S(f"row_in{layer}{s}"), 16)

        def gather(pool, table, layer):
            with pool.Fori(0, groups // U) as j:
                for s in range(U):
                    wait_alone(pool, pool_waits, S(f"src_in{layer}{s}"), j * 16 + 16)
                    for t in range(T):
                        pool.indirect_dma_start(rows[s][:, t, :], None, table[:, :],
                                                bass.IndirectOffsetOnAxis(ap=src_idx[s][:, t:t + 1], axis=0))\
                            .then_inc(S(f"gathered{layer}{s}"), 16)

        with nc.Block() as block:
            @block.sync
            def _(sp):
                base, n, n_more = (sp.alloc_register(r) for r in ("sp_base", "sp_n", "sp_n_more"))
                sp.reg_mov(n_more, 0)

                def window(first):
                    rows_at = sp.snap(first, min_val=0, max_val=nodes - 1)
                    return bass.AP(xr_table.tensor, rows_at * D, [[D, P], [1, D]])

                def step(g, near):
                    if g.j is None and g.c >= groups:
                        return
                    s = g.c % U
                    load_group(sp, g, 0, lambda g: sp.dma_start(
                        dst_row[s][:, 0:G + 2], bass.AP(a["dst"].tensor, g.times(G), [[0, P], [1, G + 2]])))
                    span = near(g)
                    sp.dma_start(xr_win[s][:, :], window(span[0])).then_inc(S(f"xr_in{s}"), 16)
                    sp.reg_mov(base, span[0])

                    def further():
                        sp.reg_add(base, base, P)
                        sp.reg_add(n_more, n_more, 1)
                        wait_alone(sp, sp_waits, S("xr_more_used"), sp.snap(n_more, min_val=1, max_val=1 << 20))
                        sp.dma_start(xr_more[:, :], window(base)).then_inc(S("xr_more_in"), 16)

                    further_windows(sp, n, span, further)

                sweep(sp, groups, step, spans)

            @block.gpsimd
            def _(pool):
                gather(pool, xl_table, 0)

            @block.tensor
            def _(pe):
                n, n_hide, n_in, n_sum, n_win = (pe.alloc_register(r) for r in
                                                 ("pe_n", "pe_n_hide", "pe_n_in", "pe_n_sum", "pe_n_win"))
                for r in (n_hide, n_in, n_sum, n_win):
                    pe.reg_mov(r, 0)
                count = lambda r: pe.snap(r, min_val=1, max_val=1 << 20)
                pe.sem_inc(S("xr_more_used"), 1)
                pe.sem_inc(S("node_more_used"), 1)
                pe.sem_inc(S("edge_more_used"), 1)

                def sources(g):
                    s, h = g.c % U, ph[g.c % 2]
                    wait_alone(pe, pe_waits, S(f"gathered0{s}"), g.use(16 * T, 16 * T))
                    if g.at_least(2):
                        pe.wait_ge(S("relu_ready"), g.times(2, -2))
                    for t in range(T):
                        pe.matmul(h[:, t, :], rows[s][:, t, :], ident[:, :], start=(t % 4 == 0), stop=False)

                def targets(g, span):
                    s, h = g.c % U, ph[g.c % 2]

                    def product(xr_of, one_hot, stop):
                        by_tile = one_hot.rearrange("n (p t) -> n t p", t=T)
                        return [pe.matmul(h[:, k:k + 4, :], xr_of[:, :], by_tile[:, k:k + 4, :], start=False, stop=stop)
                                for k in range(0, T, 4)]

                    def further():
                        pe.reg_add(n_hide, n_hide, 1)
                        pe.reg_add(n_in, n_in, 16)
                        wait_alone(pe, pe_waits, S("node_more_made"), count(n_hide))
                        pe.wait_ge(S("xr_more_in"), count(n_in))
                        product(xr_more, node_more, False)[-1].then_inc(S("xr_more_used"), 1)
                        wait_alone(pe, pe_waits, S("xr_more_used"), count(n_hide) + 1)
                        pe.sem_inc(S("node_more_used"), 1)

                    further_windows(pe, n, span, further)
                    pe.wait_ge(S(f"xr_in{s}"), g.use(16, 16))
                    pe.wait_ge(S("node_of_made"), g.times(1, 1))
                    for ins in product(xr_win[s], node_of[g.c % 2][:, :], True):
                        ins.then_inc(S("h_ready"), 1)

                def attend(g):
                    if g.at_least(1):
                        pe.wait_ge(S("shifted_ready"), g.times(1, 0))
                    out_t = logit_all.rearrange("p (h t) -> p t h", t=T)
                    for t in range(T):
                        if t % 4 == 0:
                            pe.wait_ge(S("relu_ready"), g.times(2, 1 + t // 4))
                        pe.matmul(out_t[:, t, :], relu_h[0][:, t, :], att_heads[:, :], start=(t == 0), stop=False)
                        ins = pe.matmul(out_t[:, t, :], relu_h[1][:, t, :], att_heads[:, :], start=False, stop=(t == T - 1))
                    ins.then_inc(S("logit_ready"), 1)

                def sum_up(g, span):
                    w = wmsg[g.c % 2]

                    def visit(k):
                        pe.reg_add(n_win, n_win, 1)
                        for t in range(T):
                            ins = pe.matmul(pA[k][:, 0:WC], edge_of[k][:, t, :], w[:, t, :],
                                            start=(t == 0), stop=(t == T - 1 and k == 1))
                        return ins

                    def further():
                        pe.reg_add(n_sum, n_sum, 1)
                        wait_alone(pe, pe_waits, S("edge_more_made"), count(n_sum))
                        pe.wait_ge(S("win_ready"), count(n_win))
                        visit(1).then_inc(S("edge_more_used"), 1)
                        wait_alone(pe, pe_waits, S("edge_more_used"), count(n_sum) + 1)
                        pe.sem_inc(S("summed"), 1)

                    pe.wait_ge(S("edge_of_made"), g.times(1, 1))
                    visit(0)
                    pe.matmul(pA[0][:, 0:WC], first_row[0:1, :], carried[0:1, :], start=False, stop=True)\
                      .then_inc(S("summed"), 1)
                    further_windows(pe, n, span, further)

                def pick_last(g):
                    wait_alone(pe, pe_waits, S("win_ready"), count(n_win))
                    pe.matmul(pick, last_node[:, g.c % U:g.c % U + 1], win[:, :], start=True, stop=True)\
                      .then_inc(S("picked"), 1)

                for _ in range(24):
                    pe.matmul(pA[0][:, 0:P], ident[:, :], ident[:, :], start=True, stop=True)

                def step(g, near):
                    more = not (g.j is None and g.c >= groups)
                    beyond = not (g.j is None and g.c + 1 >= groups)
                    if not g.at_least(1):
                        sources(g)
                        targets(g, near(g))
                        attend(g)
                    if more:
                        pe.wait_ge(S("run_ready"), g.times(1, 1))
                        run_h = by_head(run)
                        pe.transpose(pT1[0:H, 0:P], run_h[:, :, T - 1], ident[:, :])
                        pe.transpose(pT1[0:H, P:2 * P], run_h[:, :, 0], ident[:, :]).then_inc(S("ends_across"), 1)
                    if beyond:
                        sources(g + 1)
                        targets(g + 1, near(g + 1))
                    if more:
                        wait_alone(pe, pe_waits, S("carry_ready"), g.times(1, 1))
                        pe.transpose(pT2[:, 0:H], carry_f[:, 0:P], ident[0:H, 0:H])
                        pe.transpose(pT2[:, H:2 * H], carry_b[:, 1:P + 1], ident[0:H, 0:H])\
                          .then_inc(S("carry_back"), 1)
                    if g.at_least(1):
                        sum_up(g + -1, near(g + -1))
                    if beyond:
                        attend(g + 1)
                    if g.at_least(1):
                        pick_last(g + -1)

                sweep(pe, groups, step, spans)

            @block.scalar
            def _(act):
                n, n_win, n_out, node = (act.alloc_register(r) for r in ("act_n", "act_n_win", "act_n_out", "act_node"))
                act.reg_mov(n_win, 0)
                act.reg_mov(n_out, 0)
                count = lambda r: act.snap(r, min_val=1, max_val=1 << 20)
                zeros = bass.AP(sums_table.tensor, 0, [[WC, P], [P * WC, blocks + 1], [1, WC]])
                act.dma_start(zeros, win[:, :].unsqueeze(1).to_broadcast([P, blocks + 1, WC]))\
                   .then_inc(S("win_out"), 16)

                def relu(g):
                    for half, k in enumerate(range(0, T, 4)):
                        h = ph[g.c % 2][:, k:k + 4, :]
                        act.wait_ge(S("h_ready"), g.times(2, half + 1))
                        act.activation(relu_h[0][:, k:k + 4, :], h, ACT.Relu, scale=1.0 - GAT_SLOPE)
                        act.activation(relu_h[1][:, k:k + 4, :], h, ACT.Copy, scale=GAT_SLOPE)\
                           .then_inc(S("relu_ready"), 1)

                def keep(span):
                    def visit(k):
                        act.reg_add(n_win, n_win, 1)
                        act.reg_add(n_out, n_out, 16)
                        act.wait_ge(S("summed"), count(n_win))
                        act.wait_ge(S("win_out"), count(n_out))
                        act.activation(win[:, :], pA[k][:, 0:WC], ACT.Copy).then_inc(S("win_ready"), 1)
                        act.wait_ge(S("win_ready"), count(n_win))
                        at = act.snap(node, min_val=0, max_val=nodes - 1)
                        act.dma_start(bass.AP(sums_table.tensor, at * WC, [[WC, P], [1, WC]]), win[:, :])\
                           .then_inc(S("win_out"), 16)

                    def further():
                        act.reg_add(node, node, P)
                        visit(1)

                    act.reg_mov(node, span[0])
                    visit(0)
                    further_windows(act, n, span, further)

                def step(g, near):
                    if not g.at_least(1):
                        relu(g)
                    if not (g.j is None and g.c + 1 >= groups):
                        relu(g + 1)
                    if g.at_least(1):
                        keep(near(g + -1))
                    if not (g.j is None and g.c >= groups):
                        act.wait_ge(S("shifted_ready"), g.times(1, 1))
                        heads = wmsg[g.c % 2][:, :, 0:H * HC].rearrange("p t (h k) -> p t h k", k=HC)
                        act.activation(heads[:, :, :, C], shifted[:, :, 0:T].rearrange("p h t -> p t h"), ACT.Exp)
                        act.activation(r_exp[:, :], shifted[:, :, T], ACT.Exp).then_inc(S("weights_ready"), 1)

                sweep(act, groups, step, spans)
                act.reg_add(n_out, n_out, 16)
                wait_alone(act, act_waits, S("win_out"), count(n_out))

            @block.vector
            def _(v):
                n, n_hide, n_hide_link, n_sum, n_sum_link = (v.alloc_register(r) for r in (
                    "v_n", "v_n_hide", "v_n_hide_link", "v_n_sum", "v_n_sum_link"))
                for r in (n_hide, n_hide_link, n_sum, n_sum_link):
                    v.reg_mov(r, 0)
                count = lambda r: v.snap(r, min_val=1, max_val=1 << 20)
                for s in range(U):
                    v.sem_inc(S(f"rows_free0{s}"), 1)
                v.sem_inc(S("dst_taken0"), U)
                soft, hide = Chain(v, S("soft_chain")), Chain(v, S("hide_chain"))

                def node_one_hot(g):
                    s = g.c % U
                    first, ids = first_node[:, s:s + 1], dst_row[s][:, 1:1 + G]
                    v.wait_ge(S(f"row_in0{s}"), g.use(16, 16))
                    hide.at(g.times(HIDE_LINKS))
                    hide.link(v.tensor_tensor(first, node_id[:, 0:1], dst_row[s][:, 1:2], ALU.add))
                    if g.at_least(2):
                        v.wait_ge(S("h_ready"), g.times(2, -2))
                    v.tensor_scalar(node_of[g.c % 2][:, :], ids, first, None, ALU.is_equal)\
                     .then_inc(S("node_of_made"), 1)

                def further_one_hots(g, span):
                    s = g.c % U
                    first, ids = first_node[:, s:s + 1], dst_row[s][:, 1:1 + G]

                    def further():
                        v.reg_add(n_hide, n_hide, 1)
                        wait_alone(v, v_waits, S("node_more_used"), count(n_hide))
                        v.tensor_scalar(first, first, float(P), None, ALU.add).then_inc(S("more_chain"), 1)
                        v.wait_ge(S("more_chain"), count(n_hide))
                        v.tensor_scalar(node_more, ids, first, None, ALU.is_equal).then_inc(S("node_more_made"), 1)
                        wait_alone(v, v_waits, S("node_more_made"), count(n_hide))

                    wait_alone(v, v_waits, S("node_of_made"), g.times(1, 1))
                    further_windows(v, n, span, further)
                    v.tensor_tensor(last_node[:, s:s + 1], first, dst_row[s][:, G:G + 1], ALU.is_equal)

                def prepare(g):
                    s = g.c % U
                    soft.at(g.times(SOFT_LINKS))
                    v.wait_ge(S(f"near_in0{s}"), g.use(16, 16))
                    soft.link(v.tensor_scalar(dst_big[:, :], dst_near[s][:, :], BIG, None, ALU.mult))
                    v.tensor_tensor(by_head(step_pen)[:, :, 1:T], dst_big[:, 1:T].unsqueeze(1).to_broadcast([P, H, T - 1]),
                                    dst_big[:, 2:T + 1].unsqueeze(1).to_broadcast([P, H, T - 1]), ALU.subtract)
                    v.tensor_scalar(pen_first[:, :], dst_big[:, 1:T + 1], dst_big[:, 0:1], -1.0,
                                    ALU.subtract, ALU.mult)
                    v.tensor_scalar(pen_last[:, :], dst_big[:, 1:T + 1], dst_big[:, T + 1:T + 2], None, ALU.subtract)
                    v.tensor_tensor(is_last[:, :], dst_big[:, 1:T + 1], dst_big[:, 2:T + 2], ALU.not_equal)
                    ahead = dst_row[s][0:H, 0:G].rearrange("h (p e) -> h e p", e=T)[:, 0:2, :]
                    behind = dst_row[s][0:H, T:G + T].rearrange("h (p e) -> h e p", e=T)[:, 0:2, :]
                    soft.link(v.tensor_tensor(row_pen[:, :, :], ahead, behind, ALU.subtract))
                    soft.link(v.tensor_scalar(row_pen[:, :, :], row_pen[:, :, :], BIG, None, ALU.mult))
                    assert soft.n == PREPARE_LINKS

                def maxima(g):
                    soft.at(g.times(SOFT_LINKS), PREPARE_LINKS)
                    v.wait_ge(S("logit_ready"), g.times(1, 1))
                    soft.link(v.tensor_tensor_scan(fwd[:, :], step_pen[:, 0:H * T], logit, -BIG,
                                                   ALU.add, ALU.max))
                    v.tensor_tensor_scan(run[:, ::-1], step_pen[:, :0:-1], fwd[:, ::-1], -BIG,
                                         ALU.add, ALU.max).then_inc(S("run_ready"), 1)

                def weigh(g):
                    s, w = g.c % U, wmsg[g.c % 2]
                    heads = w[:, :, 0:H * HC].rearrange("p t (h k) -> p t h k", k=HC)
                    v.wait_ge(S("weights_ready"), g.times(1, 1))
                    v.tensor_tensor(heads[:, :, :, 0:C], rows[s][:, :, :].rearrange("p t (h c) -> p t h c", h=H),
                                    heads[:, :, :, C:HC].to_broadcast([P, T, H, C]), ALU.mult)\
                     .then_inc(S(f"rows_free0{s}"), 1)
                    if g.at_least(1):
                        v.wait_ge(S("picked"), g.times(1, 0))
                        by = lambda t: t[0:1, 0:H * HC].rearrange("o (h k) -> o h k", k=HC)
                        v.tensor_tensor(by(carried), by(pick), r_exp[0:1, :].unsqueeze(2).to_broadcast([1, H, HC]),
                                        ALU.mult)

                def across(g):
                    v.wait_ge(S("ends_across"), g.times(1, 1))
                    soft.link(v.tensor_copy(carry_f[:, 0:1], carry_f[:, P:P + 1]))
                    v.tensor_tensor_scan(carry_f[:, 1:P + 1], row_pen[:, 0, :], pT1[0:H, 0:P], carry_f[:, 0:1],
                                         ALU.add, ALU.max)
                    v.tensor_tensor_scan(carry_b[:, P - 1::-1], row_pen[:, 1, ::-1], pT1[0:H, 2 * P - 1:P - 1:-1],
                                         -BIG, ALU.add, ALU.max).then_inc(S("carry_ready"), 1)

                def edge_one_hot(g, span):
                    s = g.c % U
                    v.tensor_tensor(dst_rel[:, :], dst_near[s][:, 1:T + 1], dst_row[s][:, 1:2].to_broadcast([P, T]),
                                    ALU.subtract).then_inc(S("dst_taken0"), 1)
                    v.wait_ge(S("dst_taken0"), g.times(1, U + 1))
                    one_hot = lambda k: v.tensor_tensor(edge_of[k][:, :, :], dst_rel[:, :].unsqueeze(2).to_broadcast([P, T, P]),
                                                        node_row[:, :].unsqueeze(1).to_broadcast([P, T, P]), ALU.is_equal)
                    one_hot(0).then_inc(S("edge_of_made"), 1)

                    def further():
                        v.reg_add(n_sum, n_sum, 1)
                        wait_alone(v, v_waits, S("edge_more_used"), count(n_sum))
                        v.tensor_scalar(dst_rel[:, :], dst_rel[:, :], -float(P), None, ALU.add)\
                         .then_inc(S("rel_chain"), 1)
                        v.wait_ge(S("rel_chain"), count(n_sum))
                        one_hot(1).then_inc(S("edge_more_made"), 1)
                        wait_alone(v, v_waits, S("edge_more_made"), count(n_sum))

                    wait_alone(v, v_waits, S("edge_of_made"), g.times(1, 1))
                    further_windows(v, n, span, further)

                def shift(g):
                    w = wmsg[g.c % 2]
                    v.wait_ge(S("carry_back"), g.times(1, 1))
                    v.tensor_tensor(from_f[:, :, :], pT2[:, 0:H].unsqueeze(2).to_broadcast([P, H, T]),
                                    pen_first[:, :].unsqueeze(1).to_broadcast([P, H, T]), ALU.add)
                    soft.link(v.tensor_tensor(from_b[:, :, :], pT2[:, H:2 * H].unsqueeze(2).to_broadcast([P, H, T]),
                                              pen_last[:, :].unsqueeze(1).to_broadcast([P, H, T]), ALU.add))
                    soft.link(v.tensor_tensor(top[:, :, :], from_f[:, :, :], by_head(run), ALU.max))
                    soft.link(v.tensor_tensor(top[:, :, :], top[:, :, :], from_b[:, :, :], ALU.max))
                    v.tensor_tensor(w[:, :, H * HC:WC], top[:, :, :].rearrange("p h t -> p t h"),
                                    is_last[:, :].unsqueeze(2).to_broadcast([P, T, H]), ALU.mult)
                    v.tensor_tensor(shifted[:, :, T], from_f[:, :, 0], top[:, :, 0], ALU.subtract)
                    v.tensor_tensor(shifted[:, :, 0:T], by_head(logit), top[:, :, :], ALU.subtract)\
                     .then_inc(S("shifted_ready"), 1)
                    wait_alone(v, v_waits, S("shifted_ready"), g.times(1, 1))
                    assert soft.n == SOFT_LINKS

                def step(g, near):
                    last = g + -1
                    more = not (g.j is None and g.c >= groups)
                    if not g.at_least(1):
                        node_one_hot(g)
                        further_one_hots(g, near(g))
                        node_one_hot(g + 1)
                        prepare(g)
                    if more:
                        maxima(g)
                    if not (g.j is None and g.c + 1 >= groups):
                        further_one_hots(g + 1, near(g + 1))
                    if g.at_least(1):
                        weigh(last)
                    if more:
                        across(g)
                    if g.at_least(1):
                        edge_one_hot(last, near(last))
                    if more:
                        shift(g)
                    if not (g.j is None and g.c + 2 >= groups):
                        node_one_hot(g + 2)
                    if not (g.j is None and g.c + 1 >= groups):
                        prepare(g + 1)

                sweep(v, groups, step, spans)

        def node_loop(eng, stages):
            with eng.Fori(0, pairs // UP) as j:
                for s in range(UP + max(lag for _, lag in stages)):
                    for fn, lag in stages:
                        if 0 <= s - lag < UP:
                            fn(j, s - lag)

        stat = [sb(f"stat{s}", [P, 2, 12]) for s in range(UP)]

        def layer_norm(tag, work):
            def stats(v, j, s):
                k = j * UP + (s + 1)
                for b in range(2):
                    ins = v.bn_stats(stat[s][:, b, 0:6], work[s][:, b, :])
                ins.then_inc(S(f"{tag}_stats"), 1)
                wait_alone(v, v_waits, S(f"{tag}_stats"), k)
                for b in range(2):
                    ins = v.bn_aggr(stat[s][:, b, 6:8], stat[s][:, b, 0:6])
                ins.then_inc(S(f"{tag}_var"), 1)

            def root(act, j, s):
                act.wait_ge(S(f"{tag}_var"), j * UP + (s + 1))
                act.activation(stat[s][:, :, 8], stat[s][:, :, 7], ACT.Sqrt, bias=eps[:, 0:1])\
                   .then_inc(S(f"{tag}_std"), 1)

            def scale(v, j, s):
                k = j * UP + (s + 1)
                v.wait_ge(S(f"{tag}_std"), k)
                v.reciprocal(stat[s][:, :, 9], stat[s][:, :, 8]).then_inc(S(f"{tag}_recip"), 1)
                v.wait_ge(S(f"{tag}_recip"), k)
                for b in range(2):
                    ins = v.tensor_scalar(work[s][:, b, :], work[s][:, b, :], stat[s][:, b, 6:7], stat[s][:, b, 9:10],
                                          ALU.subtract, ALU.mult)
                ins.then_inc(S(f"{tag}_normed"), 1)

            return stats, root, scale

        end_phase()

        def heads_of(t):
            return t.rearrange("p b (h c) -> p b h c", h=H)

        node_m = relu_h[0][:, :, :].rearrange("p t d -> p (t d)")[:, 0:blocks * H].rearrange("p (b h) -> p b h", h=H)
        to_exp = prod[:, :, :].rearrange("p t d -> p (t d)")[:, 0:2 * blocks * H]\
            .rearrange("p (k b h) -> p k b h", k=2, h=H)
        x_ring, xl_ring, o_ring = ring_a, ring_b, ring_c
        t_ring = [node_of[s // 4][:, 256 * (s % 4):256 * (s % 4) + 256].rearrange("p (b d) -> p b d", b=2)
                  for s in range(UP)]
        with nc.Block() as block:
            stats_a, root_a, scale_a = layer_norm("na", o_ring)
            stats_b, root_b, scale_b = layer_norm("nb", o_ring)

            @block.sync
            def _(sp):
                for k in range(pairs // UP):
                    sp.dma_start(sums[:, 2 * UP * k:2 * UP * (k + 1), :], sums_blocks[k]).then_inc(S("sums_in"), 16)
                with sp.Fori(0, pairs // UP) as j:
                    for s in range(UP):
                        sp.wait_ge(S("node_in_free"), j * UP + (s + 1))
                        sp.dma_start(x_ring[s], x_pair[j * UP + s]).then_inc(S(f"x_again{s}"), 16)
                        sp.dma_start(xl_ring[s], xl_pair[j * UP + s]).then_inc(S(f"xl_again{s}"), 16)

            @block.gpsimd
            def _(pool):
                pool.sem_inc(S("node_in_free"), UP)
                pool.memset(xr[:, :, :], 0.0)
                pool.wait_ge(S("merged"), 1)

                def selfs(j, s):
                    k = j * UP + (s + 1)
                    pool.wait_ge(S(f"xl_again{s}"), j * 16 + 16)
                    pool.wait_ge(S(f"x_again{s}"), j * 16 + 16)
                    pool.wait_ge(S("t_free"), k)
                    pool.tensor_tensor(heads_of(t_ring[s]), heads_of(xl_ring[s]),
                                       e_self_pair[:, j * UP + s].unsqueeze(3).to_broadcast([P, 2, H, C]), ALU.mult)\
                        .then_inc(S("t_made"), 1)
                    pool.wait_ge(S("t_made"), j * (2 * UP) + (2 * s + 1))
                    pool.tensor_tensor(xl_ring[s], x_ring[s], two(bias), ALU.add).then_inc(S("t_made"), 1)

                def affine(j, s):
                    k = j * UP + (s + 1)
                    pool.wait_ge(S("na_normed"), k)
                    for n, (t, op) in enumerate(((two(gamma), ALU.mult), (two(beta), ALU.add), (x_ring[s], ALU.add))):
                        pool.tensor_tensor(o_ring[s], o_ring[s], t, op).then_inc(S("affine"), 1)
                        pool.wait_ge(S("affine"), j * (3 * UP) + (3 * s + n + 1))
                    pool.sem_inc(S("node_in_free"), 1)

                node_loop(pool, [(selfs, 0), (affine, 1)])

            @block.scalar
            def _(act):
                act.wait_ge(S("merge_in"), 1)
                act.activation(to_exp, to_exp, ACT.Exp).then_inc(S("merge_exp"), 1)

                def store(j, s):
                    act.wait_ge(S("nb_normed"), j * UP + (s + 1))
                    act.dma_start(x1_pair[j * UP + s], o_ring[s]).then_inc(S(f"x1_out{s}"), 16)
                    if s == UP - 1:
                        for n in range(UP):
                            act.wait_ge(S(f"x1_out{n}"), j * 16 + 16)
                        act.sem_inc(S("x1_free"), UP)

                node_loop(act, [(lambda j, s: root_a(act, j, s), 0), (lambda j, s: root_b(act, j, s), 2), (store, 3)])

            @block.vector
            def _(v):
                n = 0

                def link(ins):
                    nonlocal n
                    n += 1
                    ins.then_inc(S("merge_chain"), 1)
                    v.wait_ge(S("merge_chain"), n)

                v.sem_inc(S("t_free"), UP)
                v.sem_inc(S("x1_free"), UP)
                den = sums[:, :, 0:H * HC].rearrange("p b (h k) -> p b h k", k=HC)[:, :, :, C]
                peak = sums[:, :, H * HC:WC]
                v.wait_ge(S("sums_in"), 16 * (pairs // UP))
                link(v.tensor_scalar(node_m, den, 0.0, -BIG, ALU.is_le, ALU.mult))
                link(v.tensor_tensor(peak, peak, node_m, ALU.add))
                link(v.tensor_tensor(node_m, peak, e_self[:, :, :], ALU.max))
                v.tensor_tensor(to_exp[:, 0], peak, node_m, ALU.subtract)
                v.tensor_tensor(to_exp[:, 1], e_self[:, :, :], node_m, ALU.subtract).then_inc(S("merge_in"), 1)
                v.wait_ge(S("merge_exp"), 1)
                link(v.tensor_tensor(node_m, den, to_exp[:, 0], ALU.mult))
                link(v.tensor_tensor(node_m, node_m, to_exp[:, 1], ALU.add))
                link(v.reciprocal(node_m, node_m))
                v.tensor_tensor(peak, to_exp[:, 0], node_m, ALU.mult)
                v.tensor_tensor(e_self[:, :, :], to_exp[:, 1], node_m, ALU.mult).then_inc(S("merged"), 1)
                v.wait_ge(S("merged"), 1)

                def combine(j, s):
                    q = j * UP + s
                    k = j * (3 * UP) + 3 * s
                    num = sums_pair[:, q, :, 0:H * HC].rearrange("p b (h k) -> p b h k", k=HC)[:, :, :, 0:C]
                    scale = sums_pair[:, q, :, H * HC:WC].unsqueeze(3).to_broadcast([P, 2, H, C])
                    v.wait_ge(S("x1_free"), j * UP + UP)
                    v.tensor_tensor(heads_of(o_ring[s]), num, scale, ALU.mult).then_inc(S("comb"), 1)
                    v.wait_ge(S("t_made"), j * (2 * UP) + (2 * s + 2))
                    v.wait_ge(S("comb"), k + 1)
                    v.tensor_tensor(o_ring[s], o_ring[s], t_ring[s], ALU.add).then_inc(S("comb"), 1)
                    v.wait_ge(S("comb"), k + 2)
                    v.tensor_tensor(o_ring[s], o_ring[s], xl_ring[s], ALU.add).then_inc(S("comb"), 1)
                    v.wait_ge(S("comb"), k + 3)
                    v.sem_inc(S("t_free"), 1)
                    stats_a(v, j, s)

                def second(j, s):
                    v.wait_ge(S("affine"), j * (3 * UP) + (3 * s + 3))
                    stats_b(v, j, s)

                node_loop(v, [(combine, 0), (lambda j, s: scale_a(v, j, s), 1), (second, 2),
                              (lambda j, s: scale_b(v, j, s), 3)])

        end_phase()

        neigh = xr
        edge_buf = [edge_of[0], edge_of[1], node_of[0][:, :].rearrange("p (t n) -> p t n", t=T)]
        attr = [dst_row[s][:, 0:G].bitcast(F32).rearrange("p (t d) -> p t d", t=T) for s in range(U)]
        msg = relu_h
        banks = [pA[0], pA[1], pT1]
        with nc.Block() as block:
            @block.sync
            def _(sp):
                def attr_load(g, parts=P):
                    src = bass.AP(a["edge_attr"].tensor, g.times(G * D), [[T * D, parts], [1, T * D]])
                    return sp.dma_start(attr[g.c % U][0:parts].rearrange("p t d -> p (t d)"), src)

                with sp.Fori(0, groups // U - 1) as j:
                    for s in range(U):
                        load_group(sp, Group(j, s), 1, attr_load)
                for n in range(groups - U, groups):
                    parts = min(P, -(-(edges - n * G) // T))
                    load_group(sp, Group(None, n), 1, lambda g: attr_load(g, parts))

            @block.gpsimd
            def _(pool):
                gather(pool, x1_table, 1)

            @block.tensor
            def _(pe):
                block_r, n_sum = pe.alloc_register("pe1_block"), pe.alloc_register("pe1_n_sum")
                pe.reg_mov(n_sum, 0)

                def visit(k, m):
                    for t in range(T):
                        ins = pe.matmul(banks[k][:, 0:D], edge_buf[k][:, t, :], m[:, t, :],
                                        start=(t == 0), stop=(t == T - 1))
                    return ins

                def step(g, near):
                    if g.j is None and g.c >= groups:
                        return

                    def further():
                        pe.reg_add(n_sum, n_sum, 1)
                        pe.wait_ge(S("again_made"), pe.snap(n_sum, min_val=1, max_val=1 << 20))
                        visit(2, msg[g.c % 2]).then_inc(S("again_summed"), 1)

                    pe.wait_ge(S("msg_made"), g.times(1, 1))
                    visit(g.c % 2, msg[g.c % 2]).then_inc(S("msg_summed"), 1)
                    further_visits(pe, block_r, near(g), further)

                sweep(pe, groups, step, bounds, 1)

            @block.vector
            def _(v):
                block_r, n_sum, n_vis = (v.alloc_register(n) for n in ("v1_block", "v1_n_sum", "v1_n_vis"))
                v.reg_mov(n_sum, 0)
                v.reg_mov(n_vis, 0)
                blk = lambda r: v.snap(r, min_val=0, max_val=blocks - 1)
                for s in range(U):
                    v.sem_inc(S(f"rows_free1{s}"), 1)
                v.sem_inc(S("dst_taken1"), U)

                def one_hot(g, k, b):
                    v.tensor_scalar(dst_rel[:, :], dst_near[g.c % U][:, 1:T + 1], block_base[:, bass.ds(blk(b), 1)], None,
                                    ALU.subtract).then_inc(S("visit1_chain"), 1)
                    v.wait_ge(S("visit1_chain"), v.snap(n_vis, min_val=0, max_val=1 << 20) + 1)
                    v.reg_add(n_vis, n_vis, 1)
                    return v.tensor_tensor(edge_buf[k][:, :, :], dst_rel[:, :].unsqueeze(2).to_broadcast([P, T, P]),
                                           node_row[:, :].unsqueeze(1).to_broadcast([P, T, P]), ALU.is_equal)

                def add(k, b):
                    v.tensor_tensor(neigh[:, blk(b), :], neigh[:, blk(b), :], banks[k][:, 0:D], ALU.add)\
                     .then_inc(S("visit1_chain"), 1)
                    v.wait_ge(S("visit1_chain"), v.snap(n_vis, min_val=0, max_val=1 << 20) + 1)
                    v.reg_add(n_vis, n_vis, 1)

                def step(g, near):
                    if not (g.j is None and g.c >= groups):
                        s = g.c % U
                        v.wait_ge(S(f"near_in1{s}"), g.use(16, 16))
                        one_hot(g, g.c % 2, near(g)[0])
                        v.wait_ge(S(f"gathered1{s}"), g.use(16 * T, 16 * T))
                        v.wait_ge(S(f"row_in1{s}"), g.use(16, 16))
                        v.tensor_tensor(msg[g.c % 2][:, :, :], rows[s][:, :, :], attr[s][:, :, :], ALU.add)\
                         .then_inc(S("msg_made"), 1)
                        v.wait_ge(S("msg_made"), g.times(1, 1))
                        v.sem_inc(S(f"rows_free1{s}"), 1)
                    if g.at_least(1):
                        last = g + -1
                        v.wait_ge(S("msg_summed"), last.times(1, 1))
                        add(last.c % 2, near(last)[0])

                        def further():
                            v.reg_add(n_sum, n_sum, 1)
                            one_hot(last, 2, block_r).then_inc(S("again_made"), 1)
                            v.wait_ge(S("again_summed"), v.snap(n_sum, min_val=1, max_val=1 << 20))
                            add(2, block_r)

                        further_visits(v, block_r, near(last), further)
                        v.sem_inc(S("dst_taken1"), 1)

                sweep(v, groups, step, bounds, 1)

        end_phase()

        x1_ring, h_ring, mlp_ring = ring_a, ring_b, ring_c
        hT_ring = t_ring
        with nc.Block() as block:
            stats_c, root_c, scale_c = layer_norm("nc", mlp_ring)

            @block.sync
            def _(sp):
                with sp.Fori(0, pairs // UP) as j:
                    for s in range(UP):
                        sp.wait_ge(S("x1_in_free"), j * UP + (s + 1))
                        sp.dma_start(x1_ring[s], x1_pair[j * UP + s]).then_inc(S(f"x1_in{s}"), 16)

            @block.gpsimd
            def _(pool):
                def residual(j, s):
                    pool.wait_ge(S("mlp_in"), j * UP + (s + 1))
                    pool.tensor_tensor(x1_ring[s], x1_ring[s], two(b2), ALU.add).then_inc(S("res_made"), 1)

                node_loop(pool, [(residual, 0)])

            @block.tensor
            def _(pe):
                def up(j, s):
                    k = j * UP + (s + 1)
                    pe.wait_ge(S("mlp_in"), k)
                    pe.wait_ge(S("hT_ready"), k)
                    for b in range(2):
                        ins = pe.transpose(pT1[:, b * P:(b + 1) * P], h_ring[s][:, b, :], ident[:, :])
                    ins.then_inc(S("h_across"), 1)
                    pe.wait_ge(S("hT_ready"), k + 1)
                    pe.wait_ge(S("z_ready"), k)
                    pe.matmul(pT2[:, 0:2 * P], w1[:, :], hT_ring[s].rearrange("p b n -> p (b n)"), start=True, stop=True)\
                      .then_inc(S("z_made"), 1)

                def down(j, s):
                    k = j * UP + (s + 1)
                    pe.wait_ge(S("act_made"), k)
                    pe.wait_ge(S("mlp_taken"), k)
                    for b in range(2):
                        ins = pe.matmul(pA[0][:, b * D:(b + 1) * D], h_ring[s][:, b, :], w2[:, :], start=True, stop=True)
                    ins.then_inc(S("mlp_ready"), 1)

                node_loop(pe, [(up, 0), (down, 1)])

            @block.scalar
            def _(act):
                act.sem_inc(S("hT_ready"), 1)
                act.sem_inc(S("z_ready"), 1)

                def up(j, s):
                    k = j * UP + (s + 1)
                    act.wait_ge(S("h_across"), k)
                    act.activation(hT_ring[s], pT1[:, 0:2 * P].rearrange("p (b n) -> p b n", b=2), ACT.Copy)\
                       .then_inc(S("hT_ready"), 1)
                    act.wait_ge(S("z_made"), k)
                    act.activation(h_ring[s], pT2[:, 0:2 * P].rearrange("p (b n) -> p b n", b=2), ACT.Identity,
                                   bias=b1[:, 0:1]).then_inc(S("z_ready"), 1)

                def store(j, s):
                    act.wait_ge(S("nc_normed"), j * UP + (s + 1))
                    act.dma_start(out_pair[j * UP + s], mlp_ring[s]).then_inc(S(f"out{s}"), 16)
                    if s == UP - 1:
                        for n in range(UP):
                            act.wait_ge(S(f"out{n}"), j * 16 + 16)
                        act.sem_inc(S("out_free"), UP)

                node_loop(act, [(up, 0), (lambda j, s: root_c(act, j, s), 2), (store, 3)])

            @block.vector
            def _(v):
                v.sem_inc(S("x1_in_free"), UP)
                v.sem_inc(S("mlp_taken"), 1)
                v.sem_inc(S("out_free"), UP)

                def mlp_in(j, s):
                    v.wait_ge(S(f"x1_in{s}"), j * 16 + 16)
                    v.scalar_tensor_tensor(h_ring[s], x1_ring[s], 2.0, split(neigh)[:, j * UP + s], ALU.mult, ALU.add)\
                     .then_inc(S("mlp_in"), 1)

                def leaky(j, s):
                    v.wait_ge(S("z_ready"), j * UP + (s + 2))
                    v.scalar_tensor_tensor(h_ring[s], h_ring[s], MLP_SLOPE, h_ring[s], ALU.mult, ALU.max)\
                     .then_inc(S("act_made"), 1)

                def residual(j, s):
                    k = j * UP + (s + 1)
                    v.wait_ge(S("out_free"), j * UP + UP)
                    v.wait_ge(S("mlp_ready"), k)
                    v.wait_ge(S("res_made"), k)
                    v.tensor_tensor(mlp_ring[s], x1_ring[s], pA[0][:, 0:2 * D].rearrange("p (b d) -> p b d", b=2), ALU.add)\
                     .then_inc(S("res_added"), 1)
                    v.wait_ge(S("res_added"), k)
                    v.sem_inc(S("mlp_taken"), 1)
                    v.sem_inc(S("x1_in_free"), 1)
                    stats_c(v, j, s)

                node_loop(v, [(mlp_in, 0), (leaky, 1), (residual, 2), (lambda j, s: scale_c(v, j, s), 3)])


def kernel(**inputs):
    import numpy as np
    import concourse.bacc as bacc
    from concourse.bass_utils import run_bass_kernel_spmd

    x = np.ascontiguousarray(inputs["x"])
    src, dst = np.asarray(inputs["src"]), np.asarray(inputs["dst"])
    n, edges = x.shape[0], src.shape[0]
    blocks = -(-(n + 1) // (2 * UP * P)) * 2 * UP
    groups = -(-edges // (U * G)) * U
    spare = groups * G - edges
    arrays = {
        "x": np.concatenate([x, np.zeros((blocks * P - n, D), x.dtype)]),
        "src": np.concatenate([src, np.zeros(spare, src.dtype)]),
        "dst": np.concatenate([np.full(1, -1, dst.dtype), dst, np.full(spare, blocks * P - 1, dst.dtype),
                               np.full(1, blocks * P, dst.dtype)]),
        "edge_attr": np.ascontiguousarray(inputs["edge_attr_128"]),
        "att": np.ascontiguousarray(inputs["L0_gnn_att"]).reshape(D),
    }
    for name, of in (("W_l", "L0_gnn_W_l"), ("W_r", "L0_gnn_W_r"), ("bias", "L0_gnn_bias"), ("gamma", "L0_gnn_ln_gamma"),
                     ("beta", "L0_gnn_ln_beta"), ("W1", "L1_gnn_W1"), ("b1", "L1_gnn_b1"), ("W2", "L1_gnn_W2"),
                     ("b2", "L1_gnn_b2")):
        arrays[name] = np.ascontiguousarray(inputs[of])
    nc = bacc.Bacc("TRN2", target_bir_lowering=False, num_devices=1)
    aps = {k: nc.dram_tensor(f"in_{k}", v.shape, mybir.dt.from_np(v.dtype), kind="ExternalInput").ap()
           for k, v in arrays.items()}
    out = nc.dram_tensor("out_x", (blocks * P, D), F32, kind="ExternalOutput").ap()
    build(nc, aps, out, edges, groups, blocks)
    r = run_bass_kernel_spmd(nc, [{f"in_{k}": v for k, v in arrays.items()}], core_ids=[0])
    return r.results[0]["out_x"][0:n]
```

```python
from contextlib import ExitStack

import concourse.bass as bass
from concourse import mybir

F32 = mybir.dt.float32
I32 = mybir.dt.int32
ALU = mybir.AluOpType
ACT = mybir.ActivationFunctionType
AX = mybir.AxisListType

P = 128
D = 128
H = 4
C = D // H
T = 8
G = P * T
U = 4
UP = 10
R = 5
HC = C + 1
WC = H * HC + H
NA = 56
BIG = 2.0 ** 112
GAT_SLOPE, MLP_SLOPE, EPS = 0.2, 0.01, 1e-5
SOFT_LINKS = 8
PREPARE_LINKS = 3
HIDE_LINKS = 1


class Group:

    def __init__(self, j, c, u=U):
        self.j, self.c, self.u = j, c, u

    def __add__(self, n):
        return Group(self.j, self.c + n, self.u)

    def times(self, a, b=0):
        return a * self.c + b if self.j is None else self.j * (self.u * a) + (a * self.c + b)

    def use(self, a, b, ring=U):
        at = a * (self.c // ring) + b
        return at if self.j is None else self.j * (a * (self.u // ring)) + at

    def at_least(self, n):
        return self.j is not None or self.c >= n


def node_loop(eng, pairs, stages):
    def steps(j, numbers):
        for c in numbers:
            for stage, lag in stages:
                if j is not None or 0 <= c - lag < pairs:
                    stage(Group(j, c - lag, UP))

    steps(None, range(UP))
    with eng.Fori(0, pairs // UP - 1) as j:
        steps(j, range(UP, 2 * UP))
    steps(None, range(pairs, pairs + max(lag for _, lag in stages)))


def sweep(eng, groups, step, ends=None, layer=0):

    def part(tag, j, first, steps, lo, n):
        regs = []
        if ends is not None:
            regs = [eng.alloc_register(f"ends{layer}_{tag}_{k}") for k in range(2 * n)]
            eng.load(regs, ends[0:1, bass.ds(2 * first if j is None else j * (2 * U), 2 * n)])
        for c in steps:
            step(Group(j, c), lambda g: (regs[2 * (g.c - lo)], regs[2 * (g.c - lo) + 1]))

    part("head", None, 0, [0], 0, 2)
    with eng.Fori(0, groups // U - 1) as j:
        part("body", j, 0, range(1, U + 1), 0, U + 2)
    base = groups - U
    part("tail", None, base, range(base + 1, groups + 1), base, U)


def further_windows(eng, n, span, body):
    eng.reg_mov(n, 1)
    with eng.While(lambda: eng.snap(n) <= eng.snap(span[1])):
        body()
        eng.reg_add(n, n, 1)


def further_visits(eng, block, ends, body):
    first, last = ends
    eng.reg_add(block, first, 1)
    with eng.While(lambda: eng.snap(block) <= eng.snap(last)):
        body()
        eng.reg_add(block, block, 1)


def wait_alone(eng, waits, sem, value):
    eng.wait_ge(sem, value)
    eng.sem_inc(waits, 1)


class Chain:

    def __init__(self, eng, sem):
        self.eng, self.sem, self.base, self.n = eng, sem, 0, 0

    def at(self, base, n=0):
        self.base, self.n = base, n

    def mark(self, ins):
        self.n += 1
        ins.then_inc(self.sem, 1)

    def link(self, ins):
        self.mark(ins)
        self.eng.wait_ge(self.sem, self.base + self.n)


def build(nc, a, out, edges, groups, blocks):
    nodes = blocks * P
    pairs = blocks // 2
    assert groups % U == 0 and groups > U and pairs % UP == 0 and pairs > UP
    assert edges % T == 0 and 0 < groups * G - edges < G
    ctx = ExitStack()
    with ctx:
        def sb(name, shape, dt=F32):
            return ctx.enter_context(nc.sbuf_tensor(name, shape, dt))

        def pb(name, shape):
            return ctx.enter_context(nc.psum_tensor(name, shape, F32))

        xl_table = nc.dram_tensor("xl_table", (nodes, D), F32, kind="Internal").ap()
        xr_table = nc.dram_tensor("xr_table", (nodes + P, D), F32, kind="Internal").ap()
        sums_table = nc.dram_tensor("sums_table", (nodes + P, WC), F32, kind="Internal").ap()
        x1_table = nc.dram_tensor("x1_table", (nodes, D), F32, kind="Internal").ap()

        ident = sb("ident", [P, P])
        iota_i = sb("iota_i", [P, P], I32)
        node_row = sb("node_row", [P, P])
        ids_i = sb("ids_i", [P, blocks], I32)
        node_id = sb("node_id", [P, blocks])
        block_base = sb("block_base", [P, blocks])
        w_lr = sb("w_lr", [P, 2 * D])
        w1, w2 = sb("w1", [P, D]), sb("w2", [P, D])
        att = sb("att", [P, D])
        att_col = sb("att_col", [P, 1])
        att_heads = sb("att_heads", [P, NA])
        first_row = sb("first_row", [1, P])
        bias, gamma, beta, b2 = (sb(n, [P, D]) for n in ("bias", "gamma", "beta", "b2"))
        b1 = sb("b1", [P, 1])
        eps = sb("eps", [P, 1])
        ends_i = sb("ends_i", [1, 2 * groups], I32)
        bounds = sb("bounds", [1, 2 * groups], I32)
        spans = sb("spans", [1, 2 * groups], I32)

        xr = sb("xr", [P, blocks, D])
        sums = sb("sums", [P, blocks, WC])
        e_self = sb("e_self", [P, blocks, H])

        src_idx = [sb(f"src_idx{s}", [P, T], I32) for s in range(U)]
        rows = [sb(f"rows{s}", [P, T, D]) for s in range(U)]
        dst_near = [sb(f"dst_near{s}", [P, T + 2], I32) for s in range(U)]
        dst_row = [sb(f"dst_row{s}", [P, G + T], I32) for s in range(U)]
        xr_win = [sb(f"xr_win{s}", [P, D]) for s in range(U)]
        xr_more = sb("xr_more", [P, D])
        node_of = [sb(f"node_of{s}", [P, G]) for s in range(2)]
        edge_of = [sb(f"edge_of{s}", [P, T, P]) for s in range(2)]
        relu_h = [sb(f"relu_h{s}", [P, T, D]) for s in range(2)]
        prod = sb("prod", [P, T, D])
        wmsg = [sb(f"wmsg{s}", [P, T, WC]) for s in range(2)]
        win = sb("win", [P, WC])
        dst_big, dst_rel = sb("dst_big", [P, T + 2]), sb("dst_rel", [P, T])
        fwd, run = sb("fwd", [P, H * T]), sb("run", [P, H * T])
        step_pen = sb("step_pen", [P, H * T + 1])
        pen_first, pen_last, is_last = (sb(n, [P, T]) for n in ("pen_first", "pen_last", "is_last"))
        row_pen = sb("row_pen", [H, 2, P])
        carry_f, carry_b = sb("carry_f", [H, P + 1]), sb("carry_b", [H, P + 1])
        from_f, from_b, top = sb("from_f", [P, H, T]), sb("from_b", [P, H, T]), sb("top", [P, H, T])
        shifted = sb("shifted", [P, H, T + 1])
        r_exp, first_node = sb("r_exp", [P, H]), sb("first_node", [P, U])
        last_node = sb("last_node", [P, U])
        carried = sb("carried", [1, WC])

        ph = [pb(f"ph{s}", [P, T, D]) for s in range(2)]
        pT1, pT2 = pb("pT1", [P, 512]), pb("pT2", [P, 512])
        pA = [pb(f"pA{s}", [P, 512]) for s in range(2)]

        def by_head(t):
            return t[:, 0:H * T].rearrange("p (h t) -> p h t", h=H)

        node_more = prod[:, :, :].rearrange("p t d -> p (t d)")
        logit_all = pT2[:, 32:32 + T * NA]
        logit = logit_all[:, 0:H * T]
        pick = pA[1][0:1, 256:256 + WC]

        pool_waits, pe_waits, v_waits, sp_waits, act_waits = (
            nc.alloc_semaphore(n) for n in ("pool_waits", "pe_waits", "v_waits", "sp_waits", "act_waits"))
        sems = {}

        def S(name):
            if name not in sems:
                sems[name] = nc.alloc_semaphore(name)
            return sems[name]

        def end_phase():
            nc.clear_and_free_semaphores(list(sems.values()))
            nc.all_engine_barrier()
            sems.clear()

        x_pair = a["x"].rearrange("(q b p) d -> q p b d", b=2, p=P)
        xl_pair = xl_table.rearrange("(q b p) d -> q p b d", b=2, p=P)
        x1_pair = x1_table.rearrange("(q b p) d -> q p b d", b=2, p=P)
        out_pair = out.rearrange("(q b p) d -> q p b d", b=2, p=P)
        xr_pairs = xr_table[0:nodes, :].rearrange("(q b p) d -> q p b d", b=2, p=P)
        sums_blocks = sums_table[0:nodes, :].rearrange("(j b p) k -> j p b k", b=2 * UP, p=P)
        def slots(t):
            flat = t[:, 0:G].bitcast(F32) if t in dst_row else \
                t[:, :, :].rearrange("p t d -> p (t d)") if len(t.shape) == 3 else t[:, :]
            return [flat[:, k:k + 2 * D].rearrange("p (b d) -> p b d", b=2) for k in range(0, G, 2 * D)]

        row_slots = slots(rows[0]) + slots(rows[1]) + slots(rows[2]) + slots(rows[3])
        ring_x, ring_a = row_slots[0:2 * R], row_slots[2 * R:3 * R]
        ring_b = (slots(edge_of[0]) + slots(edge_of[1]))[0:R]
        ring_c = (slots(node_of[0]) + slots(node_of[1]))[0:R]
        ring_d = (slots(dst_row[0]) + slots(dst_row[1]))[0:R]
        ring_e = (slots(dst_row[2]) + slots(dst_row[3]))[0:R]

        def split(t):
            return t[:, :, :].rearrange("p (q b) k -> p q b k", b=2)

        xr_pair, e_self_pair, sums_pair = split(xr), split(e_self), split(sums)

        def heads_of(t):
            return t.rearrange("p b (h c) -> p b h c", h=H)

        def two(t):
            return t[:, :].unsqueeze(1).to_broadcast([P, 2, D])

        with nc.Block() as block:
            @block.sync
            def _(sp):
                for t, n in ((w_lr[:, 0:D], "W_l"), (w_lr[:, D:2 * D], "W_r"), (w1[:, :], "W1"), (w2[:, :], "W2")):
                    sp.dma_start(t, a[n]).then_inc(S("consts_in"), 16)
                sp.dma_start(att_col[:, :], a["att"].rearrange("(p o) -> p o", o=1)).then_inc(S("consts_in"), 16)
                for t, n in ((att, "att"), (bias, "bias"), (gamma, "gamma"), (beta, "beta"), (b2, "b2")):
                    sp.dma_start(t[:, :], a[n].partition_broadcast(P)).then_inc(S("consts_in"), 16)
                sp.dma_start(b1[:, :], a["b1"].rearrange("(p o) -> p o", o=1)).then_inc(S("consts_in"), 16)
                ends = a["dst"][1:1 + groups * G].rearrange("(o g e) -> o g e", o=1, e=G)
                end_of = ends_i[:, :].rearrange("o (g k) -> o g k", k=2)
                with nc.allow_non_contiguous_dma(reason="one number of each group"):
                    sp.dma_start(end_of[:, :, 0:1], ends[:, :, 0:1]).then_inc(S("ends_in"), 16)
                    sp.dma_start(end_of[:, :, 1:2], ends[:, :, G - 1:G]).then_inc(S("ends_in"), 16)

                def load(q):
                    if q.at_least(2 * R):
                        sp.wait_ge(S("x_taken"), q.times(1, 1 - 2 * R))
                    s = q.c % (2 * R)
                    sp.dma_start(ring_x[s], x_pair[q.times(1)]).then_inc(S(f"x_in{s}"), 16)

                def store(q):
                    sp.wait_ge(S("xr_ready"), q.times(1, 1))
                    sp.dma_start(xr_pairs[q.times(1)], xr_pair[:, q.times(1)]).then_inc(S("xr_out"), 16)

                node_loop(sp, pairs, [(load, 0), (store, 8)])
                sp.wait_ge(S("xr_out"), 16 * pairs)

            @block.gpsimd
            def _(pool):
                pool.memset(ident[:, :], 0.0).then_inc(S("ident0"), 1)
                pool.wait_ge(S("ident0"), 1)
                pool.affine_select(out=ident[:, :], in_=ident[:, :], compare_op=ALU.not_equal, fill=1.0,
                                   base=0, pattern=[[-1, P]], channel_multiplier=1).then_inc(S("ident_ready"), 1)
                pool.iota(iota_i[:, :], pattern=[[1, P]], base=0, channel_multiplier=0).then_inc(S("iota_ready"), 1)
                pool.iota(ids_i[:, :], pattern=[[P, blocks]], base=0, channel_multiplier=1)\
                    .then_inc(S("iota_ready"), 1)
                pool.wait_ge(S("consts_in"), 176)

                def weigh_self(q):
                    pool.wait_ge(S("self_ready"), q.times(1, 1))
                    l_self = ring_d[q.c % R]
                    pool.tensor_tensor(l_self, l_self, two(att), ALU.mult).then_inc(S("self_weighed"), 1)

                node_loop(pool, pairs, [(weigh_self, 0)])

            @block.tensor
            def _(pe):
                pe.wait_ge(S("ident_ready"), 1)
                pe.wait_ge(S("consts_in"), 176)

                def across(q):
                    pe.wait_ge(S(f"x_in{q.c % (2 * R)}"), q.use(16, 16, 2 * R))
                    if q.at_least(2):
                        pe.wait_ge(S("xT_ready"), q.times(1, -1))
                    for b in range(2):
                        ins = pe.transpose((pT1, pT2)[q.c % 2][:, b * P:(b + 1) * P], ring_x[q.c % (2 * R)][:, b, :],
                                           ident[:, :])
                    ins.then_inc(S("x_taken"), 1)

                def product(q):
                    pe.wait_ge(S("xT_ready"), q.times(1, 1))
                    if q.at_least(2):
                        pe.wait_ge(S("xl_ready"), q.times(1, -1))
                        pe.wait_ge(S("self_added"), q.times(1, -1))
                    for b in range(2):
                        ins = pe.matmul(pA[q.c % 2][:, b * 2 * D:(b + 1) * 2 * D], ring_a[q.c % R][:, b, :], w_lr[:, :],
                                        start=True, stop=True)
                    ins.then_inc(S("lr_ready"), 1)

                node_loop(pe, pairs, [(across, 0), (product, 1)])

            @block.scalar
            def _(act):
                act.wait_ge(S("zeros_ready"), 1)
                act.dma_start(xr_table[nodes:nodes + P, :], win[:, 0:D]).then_inc(S("pad_out"), 16)

                def copy_xT(q):
                    act.wait_ge(S("x_taken"), q.times(1, 1))
                    pT = (pT1, pT2)[q.c % 2]
                    act.activation(ring_a[q.c % R], pT[:, 0:2 * P].rearrange("p (b n) -> p b n", b=2), ACT.Copy)\
                       .then_inc(S("xT_ready"), 1)

                def copy_xl(q):
                    s = q.c % R
                    act.wait_ge(S("lr_ready"), q.times(1, 1))
                    if q.at_least(R):
                        act.wait_ge(S(f"xl_out{s}"), q.use(16, 0, R))
                    lr = pA[q.c % 2][:, :].rearrange("p (b k) -> p b k", b=2)
                    act.activation(ring_b[s], lr[:, :, 0:D], ACT.Copy).then_inc(S("xl_ready"), 1)
                    act.wait_ge(S("xl_ready"), q.times(1, 1))
                    act.dma_start(xl_pair[q.times(1)], ring_b[s]).then_inc(S(f"xl_out{s}"), 16)

                node_loop(act, pairs, [(copy_xT, 0), (copy_xl, 1)])
                act.wait_ge(S("pad_out"), 16)
                for s in range(R):
                    act.wait_ge(S(f"xl_out{s}"), 16 * (pairs // R))

            @block.vector
            def _(v):
                done = 0

                def link(ins):
                    nonlocal done
                    done += 1
                    ins.then_inc(S("node_chain"), 1)
                    v.wait_ge(S("node_chain"), done)

                v.memset(eps[:, :], EPS)
                v.memset(step_pen[:, :], -BIG)
                v.memset(win[:, :], 0.0).then_inc(S("zeros_ready"), 1)
                v.memset(carried[:, :], 0.0)
                v.memset(carry_f[:, :], -BIG)
                v.memset(carry_b[:, :], -BIG)
                v.wait_ge(S("iota_ready"), 2)
                v.tensor_copy(node_row[:, :], iota_i[:, :])
                link(v.tensor_copy(node_id[:, :], ids_i[:, :]))
                v.tensor_scalar(block_base[:, :], node_id[:, :], node_id[:, 0:1], None, ALU.subtract)
                link(v.tensor_scalar(first_row[:, :], node_row[0:1, :], 0.0, None, ALU.is_equal))
                v.wait_ge(S("ends_in"), 32)
                v.tensor_scalar(bounds[:, :], ends_i[:, :], 7, None, ALU.arith_shift_right)
                pair_of = [t[:, :].rearrange("o (g k) -> o g k", k=2) for t in (ends_i, spans)]
                link(v.tensor_copy(spans[:, :], ends_i[:, :]))
                link(v.tensor_tensor(pair_of[1][:, :, 1], pair_of[0][:, :, 1], pair_of[0][:, :, 0], ALU.subtract))
                link(v.tensor_scalar(pair_of[1][:, :, 1], pair_of[1][:, :, 1], 7, None, ALU.arith_shift_right))
                v.wait_ge(S("consts_in"), 176)
                link(v.memset(att_heads[:, :], 0.0))
                for h in range(H):
                    link(v.tensor_copy(att_heads[C * h:C * (h + 1), h:h + 1], att_col[C * h:C * (h + 1), :]))

                def hidden_self(q):
                    n = q.times(1, 1)
                    h_self = ring_d[q.c % R]
                    v.wait_ge(S("xl_ready"), n)
                    if q.at_least(R):
                        v.wait_ge(S("e_made"), q.times(1, 1 - R))
                    r = pA[q.c % 2][:, :].rearrange("p (b k) -> p b k", b=2)[:, :, D:2 * D]
                    v.tensor_copy(xr_pair[:, q.times(1)], r).then_inc(S("xr_ready"), 1)
                    v.tensor_tensor(h_self, ring_b[q.c % R], r, ALU.add).then_inc(S("self_added"), 1)
                    v.wait_ge(S("self_added"), n)
                    v.scalar_tensor_tensor(h_self, h_self, GAT_SLOPE, h_self, ALU.mult, ALU.max)\
                     .then_inc(S("self_ready"), 1)

                def sum_self(q):
                    v.wait_ge(S("self_weighed"), q.times(1, 1))
                    v.tensor_reduce(e_self_pair[:, q.times(1)], heads_of(ring_d[q.c % R]), AX.X, ALU.add)\
                     .then_inc(S("e_made"), 1)

                node_loop(v, pairs, [(hidden_self, 0), (sum_self, 2)])

        end_phase()

        def load_group(sp, g, layer, row):
            s = g.c % U
            sp.wait_ge(S(f"rows_free{layer}{s}"), g.use(1, 1))
            sp.dma_start(src_idx[s][:, :], bass.AP(a["src"].tensor, g.times(G), [[T, P], [1, T]]))\
              .then_inc(S(f"src_in{layer}{s}"), 16)
            sp.wait_ge(S(f"dst_taken{layer}"), g.times(1, 1))
            sp.dma_start(dst_near[s][:, :], bass.AP(a["dst"].tensor, g.times(G), [[T, P], [1, T + 2]]))\
              .then_inc(S(f"near_in{layer}{s}"), 16)
            row(g).then_inc(S(f"row_in{layer}{s}"), 16)

        def gather(pool, table, layer):
            with pool.Fori(0, groups // U) as j:
                for s in range(U):
                    wait_alone(pool, pool_waits, S(f"src_in{layer}{s}"), j * 16 + 16)
                    for t in range(T):
                        pool.indirect_dma_start(rows[s][:, t, :], None, table[:, :],
                                                bass.IndirectOffsetOnAxis(ap=src_idx[s][:, t:t + 1], axis=0))\
                            .then_inc(S(f"gathered{layer}{s}"), 16)

        with nc.Block() as block:
            @block.sync
            def _(sp):
                base, n, n_more = (sp.alloc_register(r) for r in ("sp_base", "sp_n", "sp_n_more"))
                sp.reg_mov(n_more, 0)

                def window(first):
                    rows_at = sp.snap(first, min_val=0, max_val=nodes - 1)
                    return bass.AP(xr_table.tensor, rows_at * D, [[D, P], [1, D]])

                def step(g, near):
                    if g.j is None and g.c >= groups:
                        return
                    s = g.c % U
                    load_group(sp, g, 0, lambda g: sp.dma_start(
                        dst_row[s][:, 0:G + 2], bass.AP(a["dst"].tensor, g.times(G), [[0, P], [1, G + 2]])))
                    span = near(g)
                    sp.dma_start(xr_win[s][:, :], window(span[0])).then_inc(S(f"xr_in{s}"), 16)
                    sp.reg_mov(base, span[0])

                    def further():
                        sp.reg_add(base, base, P)
                        sp.reg_add(n_more, n_more, 1)
                        wait_alone(sp, sp_waits, S("xr_more_used"), sp.snap(n_more, min_val=1, max_val=1 << 20))
                        sp.dma_start(xr_more[:, :], window(base)).then_inc(S("xr_more_in"), 16)

                    further_windows(sp, n, span, further)

                sweep(sp, groups, step, spans)

            @block.gpsimd
            def _(pool):
                gather(pool, xl_table, 0)

            @block.tensor
            def _(pe):
                n, n_hide, n_in, n_sum, n_win = (pe.alloc_register(r) for r in
                                                 ("pe_n", "pe_n_hide", "pe_n_in", "pe_n_sum", "pe_n_win"))
                for r in (n_hide, n_in, n_sum, n_win):
                    pe.reg_mov(r, 0)
                count = lambda r: pe.snap(r, min_val=1, max_val=1 << 20)
                pe.sem_inc(S("xr_more_used"), 1)
                pe.sem_inc(S("node_more_used"), 1)
                pe.sem_inc(S("edge_more_used"), 1)

                def sources(g):
                    s, h = g.c % U, ph[g.c % 2]
                    wait_alone(pe, pe_waits, S(f"gathered0{s}"), g.use(16 * T, 16 * T))
                    if g.at_least(2):
                        pe.wait_ge(S("relu_ready"), g.times(2, -2))
                    for t in range(T):
                        pe.matmul(h[:, t, :], rows[s][:, t, :], ident[:, :], start=(t % 4 == 0), stop=False)

                def targets(g, span):
                    s, h = g.c % U, ph[g.c % 2]

                    def product(xr_of, one_hot, stop):
                        by_tile = one_hot.rearrange("n (p t) -> n t p", t=T)
                        return [pe.matmul(h[:, k:k + 4, :], xr_of[:, :], by_tile[:, k:k + 4, :], start=False, stop=stop)
                                for k in range(0, T, 4)]

                    def further():
                        pe.reg_add(n_hide, n_hide, 1)
                        pe.reg_add(n_in, n_in, 16)
                        wait_alone(pe, pe_waits, S("node_more_made"), count(n_hide))
                        pe.wait_ge(S("xr_more_in"), count(n_in))
                        product(xr_more, node_more, False)[-1].then_inc(S("xr_more_used"), 1)
                        wait_alone(pe, pe_waits, S("xr_more_used"), count(n_hide) + 1)
                        pe.sem_inc(S("node_more_used"), 1)

                    further_windows(pe, n, span, further)
                    pe.wait_ge(S(f"xr_in{s}"), g.use(16, 16))
                    pe.wait_ge(S("node_of_made"), g.times(1, 1))
                    for ins in product(xr_win[s], node_of[g.c % 2][:, :], True):
                        ins.then_inc(S("h_ready"), 1)

                def attend(g):
                    if g.at_least(1):
                        pe.wait_ge(S("shifted_ready"), g.times(1, 0))
                    out_t = logit_all.rearrange("p (h t) -> p t h", t=T)
                    for t in range(T):
                        if t % 4 == 0:
                            pe.wait_ge(S("relu_ready"), g.times(2, 1 + t // 4))
                        pe.matmul(out_t[:, t, :], relu_h[0][:, t, :], att_heads[:, :], start=(t == 0), stop=False)
                        ins = pe.matmul(out_t[:, t, :], relu_h[1][:, t, :], att_heads[:, :], start=False, stop=(t == T - 1))
                    ins.then_inc(S("logit_ready"), 1)

                def sum_up(g, span):
                    w = wmsg[g.c % 2]

                    def visit(k):
                        pe.reg_add(n_win, n_win, 1)
                        for t in range(T):
                            ins = pe.matmul(pA[k][:, 0:WC], edge_of[k][:, t, :], w[:, t, :],
                                            start=(t == 0), stop=(t == T - 1 and k == 1))
                        return ins

                    def further():
                        pe.reg_add(n_sum, n_sum, 1)
                        wait_alone(pe, pe_waits, S("edge_more_made"), count(n_sum))
                        pe.wait_ge(S("win_ready"), count(n_win))
                        visit(1).then_inc(S("edge_more_used"), 1)
                        wait_alone(pe, pe_waits, S("edge_more_used"), count(n_sum) + 1)
                        pe.sem_inc(S("summed"), 1)

                    pe.wait_ge(S("edge_of_made"), g.times(1, 1))
                    visit(0)
                    pe.matmul(pA[0][:, 0:WC], first_row[0:1, :], carried[0:1, :], start=False, stop=True)\
                      .then_inc(S("summed"), 1)
                    further_windows(pe, n, span, further)

                def pick_last(g):
                    wait_alone(pe, pe_waits, S("win_ready"), count(n_win))
                    pe.matmul(pick, last_node[:, g.c % U:g.c % U + 1], win[:, :], start=True, stop=True)\
                      .then_inc(S("picked"), 1)

                for _ in range(24):
                    pe.matmul(pA[0][:, 0:P], ident[:, :], ident[:, :], start=True, stop=True)

                def step(g, near):
                    more = not (g.j is None and g.c >= groups)
                    beyond = not (g.j is None and g.c + 1 >= groups)
                    if not g.at_least(1):
                        sources(g)
                        targets(g, near(g))
                        attend(g)
                    if more:
                        pe.wait_ge(S("run_ready"), g.times(1, 1))
                        run_h = by_head(run)
                        pe.transpose(pT1[0:H, 0:P], run_h[:, :, T - 1], ident[:, :])
                        pe.transpose(pT1[0:H, P:2 * P], run_h[:, :, 0], ident[:, :]).then_inc(S("ends_across"), 1)
                    if beyond:
                        sources(g + 1)
                        targets(g + 1, near(g + 1))
                    if more:
                        wait_alone(pe, pe_waits, S("carry_ready"), g.times(1, 1))
                        pe.transpose(pT2[:, 0:H], carry_f[:, 0:P], ident[0:H, 0:H])
                        pe.transpose(pT2[:, H:2 * H], carry_b[:, 1:P + 1], ident[0:H, 0:H])\
                          .then_inc(S("carry_back"), 1)
                    if g.at_least(1):
                        sum_up(g + -1, near(g + -1))
                    if beyond:
                        attend(g + 1)
                    if g.at_least(1):
                        pick_last(g + -1)

                sweep(pe, groups, step, spans)

            @block.scalar
            def _(act):
                n, n_win, n_out, node = (act.alloc_register(r) for r in ("act_n", "act_n_win", "act_n_out", "act_node"))
                act.reg_mov(n_win, 0)
                act.reg_mov(n_out, 0)
                count = lambda r: act.snap(r, min_val=1, max_val=1 << 20)
                zeros = bass.AP(sums_table.tensor, 0, [[WC, P], [P * WC, blocks + 1], [1, WC]])
                act.dma_start(zeros, win[:, :].unsqueeze(1).to_broadcast([P, blocks + 1, WC]))\
                   .then_inc(S("win_out"), 16)

                def relu(g):
                    for half, k in enumerate(range(0, T, 4)):
                        h = ph[g.c % 2][:, k:k + 4, :]
                        act.wait_ge(S("h_ready"), g.times(2, half + 1))
                        act.activation(relu_h[0][:, k:k + 4, :], h, ACT.Relu, scale=1.0 - GAT_SLOPE)
                        act.activation(relu_h[1][:, k:k + 4, :], h, ACT.Copy, scale=GAT_SLOPE)\
                           .then_inc(S("relu_ready"), 1)

                def keep(span):
                    def visit(k):
                        act.reg_add(n_win, n_win, 1)
                        act.reg_add(n_out, n_out, 16)
                        act.wait_ge(S("summed"), count(n_win))
                        act.wait_ge(S("win_out"), count(n_out))
                        act.activation(win[:, :], pA[k][:, 0:WC], ACT.Copy).then_inc(S("win_ready"), 1)
                        act.wait_ge(S("win_ready"), count(n_win))
                        at = act.snap(node, min_val=0, max_val=nodes - 1)
                        act.dma_start(bass.AP(sums_table.tensor, at * WC, [[WC, P], [1, WC]]), win[:, :])\
                           .then_inc(S("win_out"), 16)

                    def further():
                        act.reg_add(node, node, P)
                        visit(1)

                    act.reg_mov(node, span[0])
                    visit(0)
                    further_windows(act, n, span, further)

                def step(g, near):
                    if not g.at_least(1):
                        relu(g)
                    if not (g.j is None and g.c + 1 >= groups):
                        relu(g + 1)
                    if g.at_least(1):
                        keep(near(g + -1))
                    if not (g.j is None and g.c >= groups):
                        act.wait_ge(S("shifted_ready"), g.times(1, 1))
                        heads = wmsg[g.c % 2][:, :, 0:H * HC].rearrange("p t (h k) -> p t h k", k=HC)
                        act.activation(heads[:, :, :, C], shifted[:, :, 0:T].rearrange("p h t -> p t h"), ACT.Exp)
                        act.activation(r_exp[:, :], shifted[:, :, T], ACT.Exp).then_inc(S("weights_ready"), 1)

                sweep(act, groups, step, spans)
                act.reg_add(n_out, n_out, 16)
                wait_alone(act, act_waits, S("win_out"), count(n_out))

            @block.vector
            def _(v):
                n, n_hide, n_hide_link, n_sum, n_sum_link = (v.alloc_register(r) for r in (
                    "v_n", "v_n_hide", "v_n_hide_link", "v_n_sum", "v_n_sum_link"))
                for r in (n_hide, n_hide_link, n_sum, n_sum_link):
                    v.reg_mov(r, 0)
                count = lambda r: v.snap(r, min_val=1, max_val=1 << 20)
                for s in range(U):
                    v.sem_inc(S(f"rows_free0{s}"), 1)
                v.sem_inc(S("dst_taken0"), U)
                soft, hide = Chain(v, S("soft_chain")), Chain(v, S("hide_chain"))

                def node_one_hot(g):
                    s = g.c % U
                    first, ids = first_node[:, s:s + 1], dst_row[s][:, 1:1 + G]
                    v.wait_ge(S(f"row_in0{s}"), g.use(16, 16))
                    hide.at(g.times(HIDE_LINKS))
                    hide.link(v.tensor_tensor(first, node_id[:, 0:1], dst_row[s][:, 1:2], ALU.add))
                    if g.at_least(2):
                        v.wait_ge(S("h_ready"), g.times(2, -2))
                    v.tensor_scalar(node_of[g.c % 2][:, :], ids, first, None, ALU.is_equal)\
                     .then_inc(S("node_of_made"), 1)

                def further_one_hots(g, span):
                    s = g.c % U
                    first, ids = first_node[:, s:s + 1], dst_row[s][:, 1:1 + G]

                    def further():
                        v.reg_add(n_hide, n_hide, 1)
                        wait_alone(v, v_waits, S("node_more_used"), count(n_hide))
                        v.tensor_scalar(first, first, float(P), None, ALU.add).then_inc(S("more_chain"), 1)
                        v.wait_ge(S("more_chain"), count(n_hide))
                        v.tensor_scalar(node_more, ids, first, None, ALU.is_equal).then_inc(S("node_more_made"), 1)
                        wait_alone(v, v_waits, S("node_more_made"), count(n_hide))

                    wait_alone(v, v_waits, S("node_of_made"), g.times(1, 1))
                    further_windows(v, n, span, further)
                    v.tensor_tensor(last_node[:, s:s + 1], first, dst_row[s][:, G:G + 1], ALU.is_equal)

                def prepare(g):
                    s = g.c % U
                    soft.at(g.times(SOFT_LINKS))
                    v.wait_ge(S(f"near_in0{s}"), g.use(16, 16))
                    soft.link(v.tensor_scalar(dst_big[:, :], dst_near[s][:, :], BIG, None, ALU.mult))
                    v.tensor_tensor(by_head(step_pen)[:, :, 1:T], dst_big[:, 1:T].unsqueeze(1).to_broadcast([P, H, T - 1]),
                                    dst_big[:, 2:T + 1].unsqueeze(1).to_broadcast([P, H, T - 1]), ALU.subtract)
                    v.tensor_scalar(pen_first[:, :], dst_big[:, 1:T + 1], dst_big[:, 0:1], -1.0,
                                    ALU.subtract, ALU.mult)
                    v.tensor_scalar(pen_last[:, :], dst_big[:, 1:T + 1], dst_big[:, T + 1:T + 2], None, ALU.subtract)
                    v.tensor_tensor(is_last[:, :], dst_big[:, 1:T + 1], dst_big[:, 2:T + 2], ALU.not_equal)
                    ahead = dst_row[s][0:H, 0:G].rearrange("h (p e) -> h e p", e=T)[:, 0:2, :]
                    behind = dst_row[s][0:H, T:G + T].rearrange("h (p e) -> h e p", e=T)[:, 0:2, :]
                    soft.link(v.tensor_tensor(row_pen[:, :, :], ahead, behind, ALU.subtract))
                    soft.link(v.tensor_scalar(row_pen[:, :, :], row_pen[:, :, :], BIG, None, ALU.mult))
                    assert soft.n == PREPARE_LINKS

                def maxima(g):
                    soft.at(g.times(SOFT_LINKS), PREPARE_LINKS)
                    v.wait_ge(S("logit_ready"), g.times(1, 1))
                    soft.link(v.tensor_tensor_scan(fwd[:, :], step_pen[:, 0:H * T], logit, -BIG,
                                                   ALU.add, ALU.max))
                    v.tensor_tensor_scan(run[:, ::-1], step_pen[:, :0:-1], fwd[:, ::-1], -BIG,
                                         ALU.add, ALU.max).then_inc(S("run_ready"), 1)

                def weigh(g):
                    s, w = g.c % U, wmsg[g.c % 2]
                    heads = w[:, :, 0:H * HC].rearrange("p t (h k) -> p t h k", k=HC)
                    v.wait_ge(S("weights_ready"), g.times(1, 1))
                    v.tensor_tensor(heads[:, :, :, 0:C], rows[s][:, :, :].rearrange("p t (h c) -> p t h c", h=H),
                                    heads[:, :, :, C:HC].to_broadcast([P, T, H, C]), ALU.mult)\
                     .then_inc(S(f"rows_free0{s}"), 1)
                    if g.at_least(1):
                        v.wait_ge(S("picked"), g.times(1, 0))
                        by = lambda t: t[0:1, 0:H * HC].rearrange("o (h k) -> o h k", k=HC)
                        v.tensor_tensor(by(carried), by(pick), r_exp[0:1, :].unsqueeze(2).to_broadcast([1, H, HC]),
                                        ALU.mult)

                def across(g):
                    v.wait_ge(S("ends_across"), g.times(1, 1))
                    soft.link(v.tensor_copy(carry_f[:, 0:1], carry_f[:, P:P + 1]))
                    v.tensor_tensor_scan(carry_f[:, 1:P + 1], row_pen[:, 0, :], pT1[0:H, 0:P], carry_f[:, 0:1],
                                         ALU.add, ALU.max)
                    v.tensor_tensor_scan(carry_b[:, P - 1::-1], row_pen[:, 1, ::-1], pT1[0:H, 2 * P - 1:P - 1:-1],
                                         -BIG, ALU.add, ALU.max).then_inc(S("carry_ready"), 1)

                def edge_one_hot(g, span):
                    s = g.c % U
                    v.tensor_tensor(dst_rel[:, :], dst_near[s][:, 1:T + 1], dst_row[s][:, 1:2].to_broadcast([P, T]),
                                    ALU.subtract).then_inc(S("dst_taken0"), 1)
                    v.wait_ge(S("dst_taken0"), g.times(1, U + 1))
                    one_hot = lambda k: v.tensor_tensor(edge_of[k][:, :, :], dst_rel[:, :].unsqueeze(2).to_broadcast([P, T, P]),
                                                        node_row[:, :].unsqueeze(1).to_broadcast([P, T, P]), ALU.is_equal)
                    one_hot(0).then_inc(S("edge_of_made"), 1)

                    def further():
                        v.reg_add(n_sum, n_sum, 1)
                        wait_alone(v, v_waits, S("edge_more_used"), count(n_sum))
                        v.tensor_scalar(dst_rel[:, :], dst_rel[:, :], -float(P), None, ALU.add)\
                         .then_inc(S("rel_chain"), 1)
                        v.wait_ge(S("rel_chain"), count(n_sum))
                        one_hot(1).then_inc(S("edge_more_made"), 1)
                        wait_alone(v, v_waits, S("edge_more_made"), count(n_sum))

                    wait_alone(v, v_waits, S("edge_of_made"), g.times(1, 1))
                    further_windows(v, n, span, further)

                def shift(g):
                    w = wmsg[g.c % 2]
                    v.wait_ge(S("carry_back"), g.times(1, 1))
                    v.tensor_tensor(from_f[:, :, :], pT2[:, 0:H].unsqueeze(2).to_broadcast([P, H, T]),
                                    pen_first[:, :].unsqueeze(1).to_broadcast([P, H, T]), ALU.add)
                    soft.link(v.tensor_tensor(from_b[:, :, :], pT2[:, H:2 * H].unsqueeze(2).to_broadcast([P, H, T]),
                                              pen_last[:, :].unsqueeze(1).to_broadcast([P, H, T]), ALU.add))
                    soft.link(v.tensor_tensor(top[:, :, :], from_f[:, :, :], by_head(run), ALU.max))
                    soft.link(v.tensor_tensor(top[:, :, :], top[:, :, :], from_b[:, :, :], ALU.max))
                    v.tensor_tensor(w[:, :, H * HC:WC], top[:, :, :].rearrange("p h t -> p t h"),
                                    is_last[:, :].unsqueeze(2).to_broadcast([P, T, H]), ALU.mult)
                    v.tensor_tensor(shifted[:, :, T], from_f[:, :, 0], top[:, :, 0], ALU.subtract)
                    v.tensor_tensor(shifted[:, :, 0:T], by_head(logit), top[:, :, :], ALU.subtract)\
                     .then_inc(S("shifted_ready"), 1)
                    wait_alone(v, v_waits, S("shifted_ready"), g.times(1, 1))
                    assert soft.n == SOFT_LINKS

                def step(g, near):
                    last = g + -1
                    more = not (g.j is None and g.c >= groups)
                    if not g.at_least(1):
                        node_one_hot(g)
                        further_one_hots(g, near(g))
                        node_one_hot(g + 1)
                        prepare(g)
                    if more:
                        maxima(g)
                    if not (g.j is None and g.c + 1 >= groups):
                        further_one_hots(g + 1, near(g + 1))
                    if g.at_least(1):
                        weigh(last)
                    if more:
                        across(g)
                    if g.at_least(1):
                        edge_one_hot(last, near(last))
                    if more:
                        shift(g)
                    if not (g.j is None and g.c + 2 >= groups):
                        node_one_hot(g + 2)
                    if not (g.j is None and g.c + 1 >= groups):
                        prepare(g + 1)

                sweep(v, groups, step, spans)

        end_phase()

        stat = [sb(f"stat{s}", [P, 2, 12]) for s in range(R)]

        def layer_norm(tag, bank, result):
            def stats(v, q):
                s = stat[q.c % R]
                for b in range(2):
                    ins = v.bn_stats(s[:, b, 0:6], bank(q)[:, b * D:(b + 1) * D])
                ins.then_inc(S(f"{tag}_stats"), 1)
                wait_alone(v, v_waits, S(f"{tag}_stats"), q.times(1, 1))
                for b in range(2):
                    ins = v.bn_aggr(s[:, b, 6:8], s[:, b, 0:6])
                ins.then_inc(S(f"{tag}_var"), 1)

            def root(act, q):
                s = stat[q.c % R]
                act.wait_ge(S(f"{tag}_var"), q.times(1, 1))
                act.activation(s[:, :, 8], s[:, :, 7], ACT.Sqrt, bias=eps[:, 0:1]).then_inc(S(f"{tag}_std"), 1)

            def invert(v, q):
                s = stat[q.c % R]
                v.wait_ge(S(f"{tag}_std"), q.times(1, 1))
                v.reciprocal(s[:, :, 9], s[:, :, 8]).then_inc(S(f"{tag}_recip"), 1)
                v.wait_ge(S(f"{tag}_recip"), q.times(1, 1))
                v.scalar_tensor_tensor(s[:, :, 10], s[:, :, 6], -1.0, s[:, :, 9], ALU.mult, ALU.mult)\
                 .then_inc(S(f"{tag}_offset"), 1)

            def scale(act, q):
                s = stat[q.c % R]
                act.wait_ge(S(f"{tag}_offset"), q.times(1, 1))
                for b in range(2):
                    ins = act.activation(result(q)[:, b, :], bank(q)[:, b * D:(b + 1) * D], ACT.Identity,
                                         bias=s[:, b, 10:11], scale=s[:, b, 9:10])
                ins.then_inc(S(f"{tag}_normed"), 1)

            return stats, root, invert, scale

        node_m = relu_h[0][:, :, :].rearrange("p t d -> p (t d)")[:, 0:blocks * H].rearrange("p (b h) -> p b h", h=H)
        to_exp = prod[:, :, :].rearrange("p t d -> p (t d)")[:, 0:2 * blocks * H]\
            .rearrange("p (k b h) -> p k b h", k=2, h=H)
        xl_ring, agg_ring, self_ring, norm_ring, x1_ring = ring_a, ring_b, ring_c, ring_d, ring_e
        with nc.Block() as block:
            stats_a, root_a, invert_a, scale_a = layer_norm(
                "na", lambda q: (pT1, pT2)[q.c % 2], lambda q: norm_ring[q.c % R])
            stats_b, root_b, invert_b, scale_b = layer_norm(
                "nb", lambda q: pA[q.c % 2], lambda q: x1_ring[q.c % R])

            @block.sync
            def _(sp):
                for k in range(pairs // UP):
                    sp.dma_start(sums[:, 2 * UP * k:2 * UP * (k + 1), :], sums_blocks[k]).then_inc(S("sums_in"), 16)

                def load(q):
                    s, s2 = q.c % R, q.c % (2 * R)
                    if q.at_least(2 * R):
                        sp.wait_ge(S("out_added"), q.times(1, 1 - 2 * R))
                    sp.dma_start(ring_x[s2], x_pair[q.times(1)]).then_inc(S(f"x_again{s2}"), 16)
                    if q.at_least(R):
                        sp.wait_ge(S("self_made"), q.times(1, 1 - R))
                    sp.dma_start(xl_ring[s], xl_pair[q.times(1)]).then_inc(S(f"xl_again{s}"), 16)

                node_loop(sp, pairs, [(load, 0)])

            @block.gpsimd
            def _(pool):
                pool.memset(xr[:, :, :], 0.0)
                pool.wait_ge(S("merged"), 1)

                def from_self(q):
                    s = q.c % R
                    pool.wait_ge(S(f"xl_again{s}"), q.use(16, 16, R))
                    if q.at_least(R):
                        pool.wait_ge(S("all_added"), q.times(1, 1 - R))
                    pool.tensor_tensor(heads_of(self_ring[s]), heads_of(xl_ring[s]),
                                       e_self_pair[:, q.times(1)].unsqueeze(3).to_broadcast([P, 2, H, C]), ALU.mult)\
                        .then_inc(S("self_made"), 1)

                def by_gamma(q):
                    pool.wait_ge(S("na_normed"), q.times(1, 1))
                    pool.tensor_tensor(norm_ring[q.c % R], norm_ring[q.c % R], two(gamma), ALU.mult)\
                        .then_inc(S("gamma_made"), 1)

                node_loop(pool, pairs, [(from_self, 0), (by_gamma, 2)])

            @block.tensor
            def _(pe):
                def add_up(bank, parts):
                    for n, part in enumerate(parts):
                        ins = pe.matmul(bank[:, 0:2 * D], ident[:, :], part, start=(n == 0), stop=(n == len(parts) - 1))
                    return ins

                def combine(q):
                    s, s2 = q.c % R, q.c % (2 * R)
                    pe.wait_ge(S(f"x_again{s2}"), q.use(16, 16, 2 * R))
                    pe.wait_ge(S("self_made"), q.times(1, 1))
                    pe.wait_ge(S("agg_made"), q.times(1, 1))
                    if q.at_least(2):
                        pe.wait_ge(S("na_normed"), q.times(1, -1))
                    add_up((pT1, pT2)[q.c % 2], [ring_x[s2], two(bias), agg_ring[s], self_ring[s]])\
                        .then_inc(S("all_added"), 1)

                def residual(q):
                    pe.wait_ge(S("gamma_made"), q.times(1, 1))
                    if q.at_least(2):
                        pe.wait_ge(S("nb_normed"), q.times(1, -1))
                    add_up(pA[q.c % 2], [ring_x[q.c % (2 * R)], two(beta), norm_ring[q.c % R]])\
                        .then_inc(S("out_added"), 1)

                node_loop(pe, pairs, [(combine, 0), (residual, 3)])

            @block.scalar
            def _(act):
                act.wait_ge(S("merge_in"), 1)
                act.activation(to_exp, to_exp, ACT.Exp).then_inc(S("merge_exp"), 1)

                def scale_first(q):
                    if q.at_least(R):
                        act.wait_ge(S("out_added"), q.times(1, 1 - R))
                    scale_a(act, q)

                def finish(q):
                    s = q.c % R
                    if q.at_least(R):
                        act.wait_ge(S(f"x1_out{s}"), q.use(16, 0, R))
                    scale_b(act, q)
                    act.wait_ge(S("nb_normed"), q.times(1, 1))
                    act.dma_start(x1_pair[q.times(1)], x1_ring[s]).then_inc(S(f"x1_out{s}"), 16)

                node_loop(act, pairs, [(scale_first, 2), (lambda q: root_a(act, q), 1),
                                       (finish, 5), (lambda q: root_b(act, q), 4)])
                for s in range(R):
                    act.wait_ge(S(f"x1_out{s}"), 16 * (pairs // R))

            @block.vector
            def _(v):
                n = 0

                def link(ins):
                    nonlocal n
                    n += 1
                    ins.then_inc(S("merge_chain"), 1)
                    v.wait_ge(S("merge_chain"), n)

                den = sums[:, :, 0:H * HC].rearrange("p b (h k) -> p b h k", k=HC)[:, :, :, C]
                peak = sums[:, :, H * HC:WC]
                v.wait_ge(S("sums_in"), 16 * (pairs // UP))
                link(v.tensor_scalar(node_m, den, 0.0, -BIG, ALU.is_le, ALU.mult))
                link(v.tensor_tensor(peak, peak, node_m, ALU.add))
                link(v.tensor_tensor(node_m, peak, e_self[:, :, :], ALU.max))
                v.tensor_tensor(to_exp[:, 0], peak, node_m, ALU.subtract)
                v.tensor_tensor(to_exp[:, 1], e_self[:, :, :], node_m, ALU.subtract).then_inc(S("merge_in"), 1)
                v.wait_ge(S("merge_exp"), 1)
                link(v.tensor_tensor(node_m, den, to_exp[:, 0], ALU.mult))
                link(v.tensor_tensor(node_m, node_m, to_exp[:, 1], ALU.add))
                link(v.reciprocal(node_m, node_m))
                v.tensor_tensor(peak, to_exp[:, 0], node_m, ALU.mult)
                v.tensor_tensor(e_self[:, :, :], to_exp[:, 1], node_m, ALU.mult).then_inc(S("merged"), 1)
                v.wait_ge(S("merged"), 1)

                def aggregate(q):
                    n = q.times(1)
                    num = sums_pair[:, n, :, 0:H * HC].rearrange("p b (h k) -> p b h k", k=HC)[:, :, :, 0:C]
                    scale = sums_pair[:, n, :, H * HC:WC].unsqueeze(3).to_broadcast([P, 2, H, C])
                    if q.at_least(R):
                        v.wait_ge(S("all_added"), q.times(1, 1 - R))
                    v.tensor_tensor(heads_of(agg_ring[q.c % R]), num, scale, ALU.mult).then_inc(S("agg_made"), 1)

                def stats_first(q):
                    v.wait_ge(S("all_added"), q.times(1, 1))
                    stats_a(v, q)

                def stats_second(q):
                    v.wait_ge(S("out_added"), q.times(1, 1))
                    stats_b(v, q)

                node_loop(v, pairs, [(aggregate, 0), (lambda q: invert_a(v, q), 2), (stats_first, 1),
                                     (lambda q: invert_b(v, q), 5), (stats_second, 4)])

        end_phase()

        neigh = xr
        edge_buf = [edge_of[0], edge_of[1], node_of[0][:, :].rearrange("p (t n) -> p t n", t=T)]
        attr = [dst_row[s][:, 0:G].bitcast(F32).rearrange("p (t d) -> p t d", t=T) for s in range(U)]
        msg = relu_h
        banks = [pA[0], pA[1], pT1]
        with nc.Block() as block:
            @block.sync
            def _(sp):
                def attr_load(g, parts=P):
                    src = bass.AP(a["edge_attr"].tensor, g.times(G * D), [[T * D, parts], [1, T * D]])
                    return sp.dma_start(attr[g.c % U][0:parts].rearrange("p t d -> p (t d)"), src)

                with sp.Fori(0, groups // U - 1) as j:
                    for s in range(U):
                        load_group(sp, Group(j, s), 1, attr_load)
                for n in range(groups - U, groups):
                    parts = min(P, -(-(edges - n * G) // T))
                    load_group(sp, Group(None, n), 1, lambda g: attr_load(g, parts))

            @block.gpsimd
            def _(pool):
                gather(pool, x1_table, 1)

            @block.tensor
            def _(pe):
                block_r, n_sum = pe.alloc_register("pe1_block"), pe.alloc_register("pe1_n_sum")
                pe.reg_mov(n_sum, 0)

                def visit(k, m):
                    for t in range(T):
                        ins = pe.matmul(banks[k][:, 0:D], edge_buf[k][:, t, :], m[:, t, :],
                                        start=(t == 0), stop=(t == T - 1))
                    return ins

                def step(g, near):
                    if g.j is None and g.c >= groups:
                        return

                    def further():
                        pe.reg_add(n_sum, n_sum, 1)
                        pe.wait_ge(S("again_made"), pe.snap(n_sum, min_val=1, max_val=1 << 20))
                        visit(2, msg[g.c % 2]).then_inc(S("again_summed"), 1)

                    pe.wait_ge(S("msg_made"), g.times(1, 1))
                    visit(g.c % 2, msg[g.c % 2]).then_inc(S("msg_summed"), 1)
                    further_visits(pe, block_r, near(g), further)

                sweep(pe, groups, step, bounds, 1)

            @block.vector
            def _(v):
                block_r, n_sum, n_vis = (v.alloc_register(n) for n in ("v1_block", "v1_n_sum", "v1_n_vis"))
                v.reg_mov(n_sum, 0)
                v.reg_mov(n_vis, 0)
                blk = lambda r: v.snap(r, min_val=0, max_val=blocks - 1)
                for s in range(U):
                    v.sem_inc(S(f"rows_free1{s}"), 1)
                v.sem_inc(S("dst_taken1"), U)

                def one_hot(g, k, b):
                    v.tensor_scalar(dst_rel[:, :], dst_near[g.c % U][:, 1:T + 1], block_base[:, bass.ds(blk(b), 1)], None,
                                    ALU.subtract).then_inc(S("visit1_chain"), 1)
                    v.wait_ge(S("visit1_chain"), v.snap(n_vis, min_val=0, max_val=1 << 20) + 1)
                    v.reg_add(n_vis, n_vis, 1)
                    return v.tensor_tensor(edge_buf[k][:, :, :], dst_rel[:, :].unsqueeze(2).to_broadcast([P, T, P]),
                                           node_row[:, :].unsqueeze(1).to_broadcast([P, T, P]), ALU.is_equal)

                def add(k, b):
                    v.tensor_tensor(neigh[:, blk(b), :], neigh[:, blk(b), :], banks[k][:, 0:D], ALU.add)\
                     .then_inc(S("visit1_chain"), 1)
                    v.wait_ge(S("visit1_chain"), v.snap(n_vis, min_val=0, max_val=1 << 20) + 1)
                    v.reg_add(n_vis, n_vis, 1)

                def step(g, near):
                    if not (g.j is None and g.c >= groups):
                        s = g.c % U
                        v.wait_ge(S(f"near_in1{s}"), g.use(16, 16))
                        one_hot(g, g.c % 2, near(g)[0])
                        v.wait_ge(S(f"gathered1{s}"), g.use(16 * T, 16 * T))
                        v.wait_ge(S(f"row_in1{s}"), g.use(16, 16))
                        v.tensor_tensor(msg[g.c % 2][:, :, :], rows[s][:, :, :], attr[s][:, :, :], ALU.add)\
                         .then_inc(S("msg_made"), 1)
                        v.wait_ge(S("msg_made"), g.times(1, 1))
                        v.sem_inc(S(f"rows_free1{s}"), 1)
                    if g.at_least(1):
                        last = g + -1
                        v.wait_ge(S("msg_summed"), last.times(1, 1))
                        add(last.c % 2, near(last)[0])

                        def further():
                            v.reg_add(n_sum, n_sum, 1)
                            one_hot(last, 2, block_r).then_inc(S("again_made"), 1)
                            v.wait_ge(S("again_summed"), v.snap(n_sum, min_val=1, max_val=1 << 20))
                            add(2, block_r)

                        further_visits(v, block_r, near(last), further)
                        v.sem_inc(S("dst_taken1"), 1)

                sweep(v, groups, step, bounds, 1)

        end_phase()

        h_ring, hT_ring, out_ring = ring_a, ring_c, ring_d
        neigh_pair = split(neigh)
        flat = [t[:, :, :].rearrange("p t d -> p (t d)") for t in ph]
        hT_bank = flat[0][:, 0:2 * P]
        sum_banks = [pA[0][:, 0:2 * D], pA[1][:, 0:2 * D]] + [flat[k][:, n:n + 2 * D] for k, n in ((0, 512), (1, 0), (1, 512))]
        with nc.Block() as block:
            stats_c, root_c, invert_c, scale_c = layer_norm(
                "nc", lambda q: sum_banks[q.c % R], lambda q: out_ring[q.c % R])

            @block.sync
            def _(sp):
                def load(q):
                    s = q.c % (2 * R)
                    if q.at_least(2 * R):
                        sp.wait_ge(S("mlp_ready"), q.times(1, 1 - 2 * R))
                    sp.dma_start(ring_x[s], x1_pair[q.times(1)]).then_inc(S(f"x1_in{s}"), 16)

                node_loop(sp, pairs, [(load, 0)])

            @block.tensor
            def _(pe):
                def across(q):
                    pe.wait_ge(S("h_made"), q.times(1, 1))
                    if q.at_least(1):
                        pe.wait_ge(S("hT_ready"), q.times(1))
                    for b in range(2):
                        ins = pe.transpose(hT_bank[:, b * P:(b + 1) * P], h_ring[q.c % R][:, b, :], ident[:, :])
                    ins.then_inc(S("h_across"), 1)

                def up(q):
                    pe.wait_ge(S("hT_ready"), q.times(1, 1))
                    if q.at_least(2):
                        pe.wait_ge(S("z_ready"), q.times(1, -1))
                    pe.matmul((pT1, pT2)[q.c % 2][:, 0:2 * P], w1[:, :], hT_ring[q.c % R].rearrange("p b n -> p (b n)"),
                              start=True, stop=True).then_inc(S("z_made"), 1)

                def down(q):
                    bank = sum_banks[q.c % R]
                    pe.wait_ge(S("act_made"), q.times(1, 1))
                    if q.at_least(R):
                        pe.wait_ge(S("nc_normed"), q.times(1, 1 - R))
                    pe.matmul(bank[:, 0:2 * D], ident[:, :], ring_x[q.c % (2 * R)], start=True, stop=False)
                    pe.matmul(bank[:, 0:2 * D], ident[:, :], two(b2), start=False, stop=False)
                    for b in range(2):
                        ins = pe.matmul(bank[:, b * D:(b + 1) * D], h_ring[q.c % R][:, b, :], w2[:, :],
                                        start=False, stop=(b == 1))
                    ins.then_inc(S("mlp_ready"), 1)

                node_loop(pe, pairs, [(across, 0), (up, 1), (down, 3)])

            @block.scalar
            def _(act):
                def copy_hT(q):
                    act.wait_ge(S("h_across"), q.times(1, 1))
                    act.activation(hT_ring[q.c % R], hT_bank.rearrange("p (b n) -> p b n", b=2), ACT.Copy).then_inc(S("hT_ready"), 1)

                def add_b1(q):
                    act.wait_ge(S("z_made"), q.times(1, 1))
                    act.activation(h_ring[q.c % R], (pT1, pT2)[q.c % 2][:, 0:2 * P].rearrange("p (b n) -> p b n", b=2),
                                   ACT.Identity, bias=b1[:, 0:1]).then_inc(S("z_ready"), 1)

                def finish(q):
                    s = q.c % R
                    if q.at_least(R):
                        act.wait_ge(S(f"out{s}"), q.use(16, 0, R))
                    scale_c(act, q)
                    act.wait_ge(S("nc_normed"), q.times(1, 1))
                    act.dma_start(out_pair[q.times(1)], out_ring[s]).then_inc(S(f"out{s}"), 16)

                node_loop(act, pairs, [(copy_hT, 0), (add_b1, 1), (lambda q: root_c(act, q), 5), (finish, 7)])
                for s in range(R):
                    act.wait_ge(S(f"out{s}"), 16 * (pairs // R))

            @block.vector
            def _(v):
                def h_in(q):
                    s2 = q.c % (2 * R)
                    v.wait_ge(S(f"x1_in{s2}"), q.use(16, 16, 2 * R))
                    if q.at_least(R):
                        v.wait_ge(S("mlp_ready"), q.times(1, 1 - R))
                    v.scalar_tensor_tensor(h_ring[q.c % R], ring_x[s2], 2.0, neigh_pair[:, q.times(1)],
                                           ALU.mult, ALU.add).then_inc(S("h_made"), 1)

                def leaky(q):
                    v.wait_ge(S("z_ready"), q.times(1, 1))
                    v.scalar_tensor_tensor(h_ring[q.c % R], h_ring[q.c % R], MLP_SLOPE, h_ring[q.c % R],
                                           ALU.mult, ALU.max).then_inc(S("act_made"), 1)

                def stats(q):
                    v.wait_ge(S("mlp_ready"), q.times(1, 1))
                    stats_c(v, q)

                node_loop(v, pairs, [(h_in, 0), (leaky, 2), (stats, 4), (lambda q: invert_c(v, q), 6)])


def kernel(**inputs):
    import numpy as np
    import concourse.bacc as bacc
    from concourse.bass_utils import run_bass_kernel_spmd

    x = np.ascontiguousarray(inputs["x"])
    src, dst = np.asarray(inputs["src"]), np.asarray(inputs["dst"])
    n, edges = x.shape[0], src.shape[0]
    blocks = -(-(n + 1) // (2 * UP * P)) * 2 * UP
    groups = -(-edges // (U * G)) * U
    spare = groups * G - edges
    arrays = {
        "x": np.concatenate([x, np.zeros((blocks * P - n, D), x.dtype)]),
        "src": np.concatenate([src, np.zeros(spare, src.dtype)]),
        "dst": np.concatenate([np.full(1, -1, dst.dtype), dst, np.full(spare, blocks * P - 1, dst.dtype),
                               np.full(1, blocks * P, dst.dtype)]),
        "edge_attr": np.ascontiguousarray(inputs["edge_attr_128"]),
        "att": np.ascontiguousarray(inputs["L0_gnn_att"]).reshape(D),
    }
    for name, of in (("W_l", "L0_gnn_W_l"), ("W_r", "L0_gnn_W_r"), ("bias", "L0_gnn_bias"), ("gamma", "L0_gnn_ln_gamma"),
                     ("beta", "L0_gnn_ln_beta"), ("W1", "L1_gnn_W1"), ("b1", "L1_gnn_b1"), ("W2", "L1_gnn_W2"),
                     ("b2", "L1_gnn_b2")):
        arrays[name] = np.ascontiguousarray(inputs[of])
    nc = bacc.Bacc("TRN2", target_bir_lowering=False, num_devices=1)
    aps = {k: nc.dram_tensor(f"in_{k}", v.shape, mybir.dt.from_np(v.dtype), kind="ExternalInput").ap()
           for k, v in arrays.items()}
    out = nc.dram_tensor("out_x", (blocks * P, D), F32, kind="ExternalOutput").ap()
    build(nc, aps, out, edges, groups, blocks)
    r = run_bass_kernel_spmd(nc, [{f"in_{k}": v for k, v in arrays.items()}], core_ids=[0])
    return r.results[0]["out_x"][0:n]
```
